# Optimizing a Trainium2 kernel written in Bass

```python
import numpy as np
import jax
import jax.numpy as jnp

def _softmax(x, axis=-1):
    return jax.nn.softmax(x, axis=axis)

def _gelu(x):
    return jax.nn.gelu(x, approximate=True)

def _silu(x):
    return jax.nn.silu(x)

def _sigmoid(x):
    return jax.nn.sigmoid(x)

def _layernorm(x, axis=-1, eps=1e-05):
    m = jnp.mean(x, axis=axis, keepdims=True)
    v = jnp.var(x, axis=axis, keepdims=True)
    return (x - m) / jnp.sqrt(v + eps)

def _scatter_add(tgt, idx, src, axis=0):
    return tgt.at[idx].add(src)

def _segment_sum(src, seg, n):
    return jax.ops.segment_sum(src, seg, n)
kernel_name = 'mk_gnn_preln_d1_gnn_r8_4055bd'

def setup_inputs(seed: int=0):
    np.random.seed(seed)
    _w = jnp.asarray

    def _rec_inputs():
        import jax
        import jax.numpy as jnp
        _gk = jax.random.key(seed)
        x = -0.000202 + 1 * jax.random.normal(jax.random.fold_in(_gk, 1), (6250, 64), jnp.float32)
        src = jax.random.randint(jax.random.fold_in(_gk, 2), (200000,), 0, 6250, jnp.int32)
        dst = jax.random.randint(jax.random.fold_in(_gk, 3), (200000,), 0, 6250, jnp.int32)
        _o = jnp.argsort(dst, stable=True)
        src = src[_o]
        dst = dst[_o]
        edge_attr_64 = jax.random.uniform(jax.random.fold_in(_gk, 12), (200000, 64), jnp.float32, 0.0, 1)
        return (x, src, dst, edge_attr_64)
    x, src, dst, edge_attr_64 = _rec_inputs()

    def _L0_gnn_setup():
        import jax, jax.numpy as jnp
        import numpy as np
        N, E, D, K = (12500, 156250, 64, 64)
        key = jax.random.key(seed)
        ks = jax.random.split(key, 12)
        s = 1.0 / np.sqrt(D)
        return {'x': jax.random.normal(ks[0], (N, D), dtype=jnp.float32), 'i': jax.random.randint(ks[1], (E,), 0, N), 'j': jax.random.randint(ks[2], (E,), 0, N), 'rbf': jax.random.uniform(ks[3], (E, K), dtype=jnp.float32), 'Wf1': jax.random.uniform(ks[4], (D, K), jnp.float32, -s, s), 'bf1': jax.random.uniform(ks[5], (D,), jnp.float32, -s, s), 'Wf2': jax.random.uniform(ks[6], (D, D), jnp.float32, -s, s), 'bf2': jax.random.uniform(ks[7], (D,), jnp.float32, -s, s), 'Wl': jax.random.uniform(ks[8], (D, D), jnp.float32, -s, s), 'bl': jax.random.uniform(ks[9], (D,), jnp.float32, -s, s), 'gamma': jnp.ones((D,), jnp.float32), 'beta': jnp.zeros((D,), jnp.float32)}
    _L0_gnn_all = _L0_gnn_setup()
    _L0_gnn_in = {k: v for k, v in _L0_gnn_all.items() if k in ('Wf1', 'bf1', 'Wf2', 'bf2', 'Wl', 'bl', 'gamma', 'beta')}
    del _L0_gnn_all
    return {'x': x, 'src': src, 'dst': dst, 'edge_attr_64': edge_attr_64, 'L0_gnn_Wf1': _L0_gnn_in['Wf1'], 'L0_gnn_bf1': _L0_gnn_in['bf1'], 'L0_gnn_Wf2': _L0_gnn_in['Wf2'], 'L0_gnn_bf2': _L0_gnn_in['bf2'], 'L0_gnn_Wl': _L0_gnn_in['Wl'], 'L0_gnn_bl': _L0_gnn_in['bl'], 'L0_gnn_gamma': _L0_gnn_in['gamma'], 'L0_gnn_beta': _L0_gnn_in['beta']}

def reference(x, src, dst, edge_attr_64, L0_gnn_Wf1, L0_gnn_bf1, L0_gnn_Wf2, L0_gnn_bf2, L0_gnn_Wl, L0_gnn_bl, L0_gnn_gamma, L0_gnn_beta):
    import jax
    import jax.numpy as jnp

    def _L0_gnn_ref(x, i, j, rbf, Wf1, bf1, Wf2, bf2, Wl, bl, gamma, beta):
        import jax, jax.numpy as jnp
        import numpy as np
        N, E, D, K = (12500, 156250, 64, 64)
        Wxh = x @ Wl.T + bl
        h = jax.nn.silu(rbf @ Wf1.T + bf1)
        f_ij = h @ Wf2.T + bf2
        msg = f_ij * Wxh[j]
        agg = jax.ops.segment_sum(msg, i, num_segments=x.shape[0])
        y = x + agg
        mu = jnp.mean(y, axis=-1, keepdims=True)
        var = jnp.var(y, axis=-1, keepdims=True)
        return (y - mu) * jax.lax.rsqrt(var + 1e-05) * gamma + beta
    h = jnp.maximum(_layernorm(x, axis=-1), 0.0)
    x = x + _L0_gnn_ref(h, src, dst, edge_attr_64, L0_gnn_Wf1, L0_gnn_bf1, L0_gnn_Wf2, L0_gnn_bf2, L0_gnn_Wl, L0_gnn_bl, L0_gnn_gamma, L0_gnn_beta)
    return x

_drawn_inputs = setup_inputs


def setup_inputs(seed=0):
    import zlib

    import numpy as np

    out = dict(_drawn_inputs(seed))
    spreads = {'L0_gnn_gamma': (1.0, 0.2), 'L0_gnn_beta': (0.0, 0.1)}
    factors = {}
    for name, (base, spread) in spreads.items():
        noise = np.random.default_rng([zlib.crc32(name.encode()), seed]).standard_normal(out[name].shape)
        drawn = base * np.exp(spread * noise) if base else spread * noise
        out[name] = jnp.asarray(drawn.astype(out[name].dtype))
    for name, factor in factors.items():
        out[name] = (out[name] * factor).astype(out[name].dtype)
    return out
```

```python
from contextlib import ExitStack

import concourse.bass as bass
from concourse import mybir

ALU = mybir.AluOpType
ACT = mybir.ActivationFunctionType
AX_X = mybir.AxisListType.X
F32 = mybir.dt.float32
I32 = mybir.dt.int32
U32 = mybir.dt.uint32

P = 128
D = 64
NODES = 6250
EDGES = 200000
TILES = 8
UNIT = TILES * P
HALF = UNIT // 2
CHUNKS = TILES // 2
UNITS = 2 * (-(-EDGES // (2 * UNIT)))
BLOCKS = UNITS // 2
W = -(-(NODES + P) // P)
W += W % 2
ROWS = W * P
EPS = 1e-5
EPI = 10

C_IDENT, C_MASK, C_SPARE = 0, P, 2 * P
CONST_COLS = 2 * P + 1
V_W1, V_W2, V_WL, V_GAMMA, V_BETA, V_B1 = 0, P, 2 * P, 3 * P, 3 * P + D, 3 * P + 2 * D
VALUE_COLS = V_B1 + 1
R_B2, R_BL, R_ONES = 0, TILES * D, 2 * TILES * D
ROW_COLS = R_ONES + P


def build(nc, x_in, attr_in, index_in, const_in, value_in, row_in, out):
    with ExitStack() as ctx:
        def sb(name, shape, dt=F32):
            return ctx.enter_context(nc.sbuf_tensor(name, shape, dt))

        def psum(name, cols=512):
            return ctx.enter_context(nc.psum_tensor(name, [P, cols], F32))

        def sem(name):
            return ctx.enter_context(nc.semaphore(name))

        def pair(make):
            return [make(u) for u in range(2)]

        wxh_dram = nc.dram_tensor("wxh_rows", (ROWS, D), F32, kind="Internal").ap()
        sums_dram = [nc.dram_tensor(f"sums{j}", (ROWS, D), F32, kind="Internal").ap() for j in range(TILES)]

        x = sb("x", [P, W, D])
        h = sb("h", [P, W, D])
        work = sb("work", [P, W, D])
        square = sb("square", [P, W, D])
        stat = sb("stat", [P, 4, W])
        hT = pair(lambda u: sb(f"hT{u}", [P, 512]))
        const = sb("const", [P, CONST_COLS])
        value = sb("value", [P, VALUE_COLS])
        row = sb("row", [1, ROW_COLS])
        eps = sb("eps", [P, 1])
        attr = pair(lambda u: sb(f"attr{u}", [P, HALF]))
        index = pair(lambda u: sb(f"index{u}", [P, 2 * TILES], I32))
        src = pair(lambda u: sb(f"src{u}", [P, TILES]))
        hidden = pair(lambda u: sb(f"hidden{u}", [P, HALF]))
        gathered = pair(lambda u: sb(f"gathered{u}", [P, TILES, D]))
        msg = pair(lambda u: sb(f"msg{u}", [P, TILES, D]))
        last_match = pair(lambda u: sb(f"last_match{u}", [P, TILES, P]))
        matches = pair(lambda u: sb(f"matches{u}", [P, TILES]))
        spare = pair(lambda u: sb(f"spare{u}", [P, TILES]))
        target = pair(lambda u: sb(f"target{u}", [P, TILES], U32))
        summed = pair(lambda u: sb(f"summed{u}", [P, TILES, D]))
        parts = pair(lambda u: sb(f"parts{u}", [P, TILES, EPI, D]))

        ps_hidden = psum("ps_hidden")
        ps_filter = psum("ps_filter")
        ps_sum = psum("ps_sum")
        ps_src = pair(lambda s: psum(f"ps_src{s}"))

        ident = const[:, C_IDENT:C_IDENT + P]
        mask = const[:, C_MASK:C_MASK + P]
        spare_row = const[:, C_SPARE:C_SPARE + 1]
        w1 = value[:, V_W1:V_W1 + P]
        w2 = value[:, V_W2:V_W2 + P]
        wl = value[:, V_WL:V_WL + P]
        gamma = value[:, V_GAMMA:V_GAMMA + D]
        beta = value[:, V_BETA:V_BETA + D]
        b1 = value[:, V_B1:V_B1 + 1]
        b2 = row[:, R_B2:R_B2 + TILES * D]
        bl = row[:, R_BL:R_BL + TILES * D]
        ones = row[:, R_ONES:R_ONES + P]

        x_loaded = sem("x_loaded")
        const_loaded = sem("const_loaded")
        zeros_ready = sem("zeros_ready")
        eps_ready = sem("eps_ready")
        ln_step = sem("ln_step")
        centred = sem("centred")
        squared = sem("squared")
        variance = sem("variance")
        deviation = sem("deviation")
        h_ready = sem("h_ready")
        h_turned = sem("h_turned")
        hT_ready = sem("hT_ready")
        wxh_done = sem("wxh_done")
        wxh_copied = sem("wxh_copied")
        wxh_stored = sem("wxh_stored")
        attr_loaded = pair(lambda u: sem(f"attr_loaded{u}"))
        index_loaded = pair(lambda u: sem(f"index_loaded{u}"))
        mlp1_done = pair(lambda u: sem(f"mlp1_done{u}"))
        silu_done = pair(lambda u: sem(f"silu_done{u}"))
        src_ready = pair(lambda u: sem(f"src_ready{u}"))
        src_spread = pair(lambda s: sem(f"src_spread{s}"))
        match_built = pair(lambda s: sem(f"match_built{s}"))
        spare_done = sem("spare_done")
        target_ready = pair(lambda u: sem(f"target_ready{u}"))
        filter_done = pair(lambda u: sem(f"filter_done{u}"))
        gather_done = pair(lambda u: sem(f"gather_done{u}"))
        gather_go = sem("gather_go")
        scatter_go = sem("scatter_go")
        msg_done = sem("msg_done")
        sum_done = pair(lambda u: sem(f"sum_done{u}"))
        sum_copied = sem("sum_copied")
        settled = [sem(f"settled{j}") for j in range(TILES)]
        parts_loaded = pair(lambda u: sem(f"parts_loaded{u}"))
        parts_used = sem("parts_used")
        out_ready = sem("out_ready")
        out_stored = sem("out_stored")

        def node_rows(t):
            return t.rearrange("(p w) d -> p w d", p=P)

        BATCHES = [(w0, min(w0 + 8, W)) for w0 in range(0, W, 8)]
        EPILOGUE = W // EPI

        block = ctx.enter_context(nc.Block())

        @block.sync
        def _(sp):
            sp.dma_start(x[:], node_rows(x_in)).then_inc(x_loaded, 16)
            sp.dma_start(const[:], const_in).then_inc(const_loaded, 16)
            sp.dma_start(value[:], value_in).then_inc(const_loaded, 16)
            sp.dma_start(row[:], row_in).then_inc(const_loaded, 16)

            def load(g, u, free=None):
                if free is not None:
                    sp.wait_ge(mlp1_done[u], free)
                    sp.wait_ge(gather_done[u], free * 16 * TILES)
                    sp.wait_ge(src_ready[u], free)
                sp.dma_start(attr[u][:], attr_in[g]).then_inc(attr_loaded[u], 16)
                sp.dma_start(index[u][:], index_in[g]).then_inc(index_loaded[u], 16)

            load(0, 0)
            load(1, 1)
            sp.wait_ge(wxh_copied, len(BATCHES))
            sp.dma_start(node_rows(wxh_dram), work[:]).then_inc(wxh_stored, 16)
            with sp.Fori(0, BLOCKS - 1) as b:
                for u in range(2):
                    load(2 * b + 2 + u, u, free=b + 1)

            for j in range(TILES):
                sp.wait_ge(settled[j], 16 * (UNITS + 1))
            for n in range(EPILOGUE):
                if n >= 2:
                    sp.wait_ge(parts_used, n - 1)
                for j in range(TILES):
                    sp.dma_start(parts[n % 2][:, j], node_rows(sums_dram[j])[:, n * EPI:(n + 1) * EPI]
                                 ).then_inc(parts_loaded[n % 2], 16)
            sp.wait_ge(out_ready, EPILOGUE)
            sp.dma_start(node_rows(out), work[:]).then_inc(out_stored, 16)
            sp.wait_ge(out_stored, 16)

        @block.gpsimd
        def _(pool):
            nc.gpsimd.memset(eps[:], EPS).then_inc(eps_ready, 1)
            nc.gpsimd.memset(square[:], 0.0).then_inc(zeros_ready, 1)
            pool.wait_ge(zeros_ready, 1)
            for j in range(TILES):
                pool.dma_start(node_rows(sums_dram[j]), square[:]).then_inc(settled[j], 16)

            def gather(u, n):
                pool.wait_ge(index_loaded[u], 16 * n)
                pool.wait_ge(sum_done[u], n - 1)
                pool.sem_inc(gather_go, 1)
                for j in range(TILES):
                    pool.indirect_dma_start(
                        gathered[u][:, j], None, wxh_dram,
                        bass.IndirectOffsetOnAxis(ap=index[u][:, TILES + j:TILES + j + 1].bitcast(U32), axis=0),
                    ).then_inc(gather_done[u], 16)

            def scatter(u, n, g):
                pool.wait_ge(target_ready[u], n)
                pool.wait_ge(sum_copied, g + 1)
                for j in range(TILES):
                    pool.wait_ge(settled[j], 16 * (g + 1))
                    pool.sem_inc(scatter_go, 1)
                    pool.indirect_dma_start(
                        sums_dram[j], bass.IndirectOffsetOnAxis(ap=target[u][:, j:j + 1], axis=0),
                        summed[u][:, j], None, compute_op=ALU.add).then_inc(settled[j], 16)

            pool.wait_ge(wxh_stored, 16)
            gather(0, 1)
            with pool.Fori(0, BLOCKS - 1) as b:
                gather(1, b + 1)
                scatter(0, b + 1, 2 * b)
                gather(0, b + 2)
                scatter(1, b + 1, 2 * b + 1)
            gather(1, BLOCKS)
            scatter(0, BLOCKS, UNITS - 2)
            scatter(1, BLOCKS, UNITS - 1)

        def project(pe, n):
            w0, w1_ = BATCHES[n]
            cols = (w1_ - w0) * D
            acc = [ps_hidden, ps_filter][n % 2]
            pe.wait_ge(hT_ready, n + 1)
            if n >= 2:
                pe.wait_ge(wxh_copied, n - 1)
            nc.tensor.matmul(acc[:, :cols], ones, bl[:, :cols], start=True, stop=False)
            for k in range(cols // P):
                last = nc.tensor.matmul(acc[:, k * P:(k + 1) * P], hT[n % 2][:, k * P:(k + 1) * P], wl,
                                        start=False, stop=(k == cols // P - 1))
            last.then_inc(wxh_done, 1)

        def edge_unit_pe(pe, u, b):
            g = 2 * b + u
            pe.wait_ge(src_ready[u], b + 1)
            for s in range(2):
                pe.wait_ge(match_built[s], g)
                for k in range(4):
                    j = 4 * s + k
                    last = nc.tensor.transpose(ps_src[s][:, k * P:(k + 1) * P],
                                               src[u][:, j:j + 1].to_broadcast([P, P]), ident)
                last.then_inc(src_spread[s], 1)
            pe.wait_ge(attr_loaded[u], 16 * (b + 1))
            pe.wait_ge(silu_done[1 - u], b + u)
            nc.tensor.matmul(ps_hidden[:], w1, attr[u][:], start=True, stop=True).then_inc(mlp1_done[u], 1)
            pe.wait_ge(msg_done, g)
            nc.tensor.matmul(ps_filter[:], ones, b2, start=True, stop=False)
            pe.wait_ge(silu_done[u], b + 1)
            for k in range(CHUNKS):
                last = nc.tensor.matmul(ps_filter[:, k * P:(k + 1) * P], hidden[u][:, k * P:(k + 1) * P], w2,
                                        start=False, stop=(k == CHUNKS - 1))
            last.then_inc(filter_done[u], 1)
            pe.wait_ge(sum_copied, g)
            pe.wait_ge(msg_done, g + 1)
            pe.wait_ge(match_built[0], g + 1)
            pe.wait_ge(match_built[1], g + 1)
            for j in range(TILES):
                last = nc.tensor.matmul(ps_sum[:, j * D:(j + 1) * D], last_match[u][:, j], msg[u][:, j],
                                        start=True, stop=True)
            last.then_inc(sum_done[u], 1)

        @block.tensor
        def _(pe):
            pe.wait_ge(const_loaded, 48)
            pe.wait_ge(h_ready, 1)
            for n, (w0, w1_) in enumerate(BATCHES):
                if n >= 2:
                    pe.wait_ge(hT_ready, n - 1)
                for k in range((w1_ - w0) // 2):
                    last = nc.tensor.transpose([ps_src[0], ps_src[1]][n % 2][:, k * P:(k + 1) * P],
                                               h[:, w0 + 2 * k:w0 + 2 * k + 2, :].rearrange("p w d -> p (w d)"),
                                               ident)
                last.then_inc(h_turned, 1)
                if n >= 1:
                    project(pe, n - 1)
            project(pe, len(BATCHES) - 1)

            pe.wait_ge(wxh_copied, len(BATCHES))
            with pe.Fori(0, BLOCKS) as b:
                for u in range(2):
                    edge_unit_pe(pe, u, b)

        @block.scalar
        def _(act):
            act.wait_ge(centred, 1)
            act.wait_ge(settled[0], 16)
            for j in range(1, TILES):
                act.wait_ge(settled[j], 16)
            nc.scalar.activation(square[:], work[:], ACT.Square).then_inc(squared, 1)
            act.wait_ge(variance, 1)
            act.wait_ge(eps_ready, 1)
            nc.scalar.activation(stat[:, 3], stat[:, 2], ACT.Sqrt, bias=eps[:], scale=1.0 / D).then_inc(deviation, 1)
            for n, (w0, w1_) in enumerate(BATCHES):
                act.wait_ge(wxh_done, n + 1)
                nc.scalar.copy(work[:, w0:w1_, :].rearrange("p w d -> p (w d)"),
                               [ps_hidden, ps_filter][n % 2][:, :(w1_ - w0) * D]).then_inc(wxh_copied, 1)
            with act.Fori(0, BLOCKS) as b:
                for u in range(2):
                    g = 2 * b + u
                    act.wait_ge(mlp1_done[u], b + 1)
                    act.wait_ge(filter_done[u], b)
                    nc.scalar.activation(hidden[u][:], ps_hidden[:], ACT.Silu, bias=b1).then_inc(silu_done[u], 1)
                    act.wait_ge(sum_done[u], b + 1)
                    for j in range(TILES):
                        act.wait_ge(settled[j], 16 * g)
                    nc.scalar.copy(summed[u][:].rearrange("p j d -> p (j d)"), ps_sum[:]).then_inc(sum_copied, 1)
            for n in range(EPILOGUE):
                part = slice(n * EPI, (n + 1) * EPI)
                act.wait_ge(centred, n + 2)
                nc.scalar.activation(square[:, part], work[:, part], ACT.Square).then_inc(squared, 1)
                act.wait_ge(variance, n + 2)
                nc.scalar.activation(stat[:, 3, part], stat[:, 2, part], ACT.Sqrt, bias=eps[:],
                                     scale=1.0 / D).then_inc(deviation, 1)

        @block.vector
        def _(dve):
            steps = [0]

            def then_next(ins):
                steps[0] += 1
                ins.then_inc(ln_step, 1)
                dve.wait_ge(ln_step, steps[0])

            def wide(column, n):
                return column.rearrange("p (w o) -> p w o", o=1).to_broadcast([P, n, D])

            def normalise(part, y, n):
                cols = part.stop - part.start
                then_next(nc.vector.tensor_reduce(stat[:, 0, part], y, AX_X, ALU.add))
                then_next(nc.vector.tensor_scalar(stat[:, 1, part], stat[:, 0, part], -1.0 / D, None, ALU.mult))
                nc.vector.tensor_tensor(work[:, part], y, wide(stat[:, 1, part], cols), ALU.add).then_inc(centred, 1)
                dve.wait_ge(squared, n + 1)
                nc.vector.tensor_reduce(stat[:, 2, part], square[:, part], AX_X, ALU.add).then_inc(variance, 1)
                dve.wait_ge(deviation, n + 1)
                then_next(nc.vector.reciprocal(stat[:, 0, part], stat[:, 3, part]))

            dve.wait_ge(x_loaded, 16)
            whole = slice(0, W)
            normalise(whole, x[:], 0)
            nc.vector.scalar_tensor_tensor(out=h[:], in0=work[:], scalar=0.0, in1=wide(stat[:, 0, whole], W),
                                           op0=ALU.max, op1=ALU.mult).then_inc(h_ready, 1)
            dve.wait_ge(const_loaded, 48)
            then_next(nc.vector.tensor_tensor(x[:], x[:], beta.rearrange("p (o d) -> p o d", o=1)
                                              .to_broadcast([P, W, D]), ALU.add))
            for n, (w0, w1_) in enumerate(BATCHES):
                cols = (w1_ - w0) * D
                dve.wait_ge(h_turned, n + 1)
                if n >= 2:
                    dve.wait_ge(wxh_done, n - 1)
                nc.vector.tensor_copy(hT[n % 2][:, :cols], ps_src[n % 2][:, :cols]).then_inc(hT_ready, 1)

            with dve.Fori(0, BLOCKS) as b:
                for u in range(2):
                    g = 2 * b + u
                    dve.wait_ge(index_loaded[u], 16 * (b + 1))
                    nc.vector.tensor_copy(src[u][:], index[u][:, 0:TILES]).then_inc(src_ready[u], 1)
                    dve.wait_ge(src_ready[u], b + 1)
                    dve.wait_ge(sum_done[u], b)
                    for s in range(2):
                        dve.wait_ge(src_spread[s], g + 1)
                        for k in range(4):
                            j = 4 * s + k
                            last = nc.vector.scalar_tensor_tensor(
                                out=last_match[u][:, j], in0=ps_src[s][:, k * P:(k + 1) * P],
                                scalar=src[u][:, j:j + 1], in1=mask, op0=ALU.is_equal, op1=ALU.mult,
                                accum_out=matches[u][:, j:j + 1])
                        last.then_inc(match_built[s], 1)
                    dve.wait_ge(match_built[0], g + 1)
                    dve.wait_ge(match_built[1], g + 1)
                    nc.vector.tensor_scalar(spare[u][:], matches[u][:], 1.0, spare_row, ALU.is_gt,
                                            ALU.mult).then_inc(spare_done, 1)
                    dve.wait_ge(spare_done, g + 1)
                    for j in range(TILES):
                        dve.wait_ge(settled[j], 16 * g)
                    nc.vector.tensor_tensor(target[u][:], spare[u][:], src[u][:], ALU.max
                                            ).then_inc(target_ready[u], 1)
                    dve.wait_ge(filter_done[u], b + 1)
                    dve.wait_ge(gather_done[u], 16 * TILES * (b + 1))
                    nc.vector.tensor_tensor(msg[u][:].rearrange("p j d -> p (j d)"), ps_filter[:],
                                            gathered[u][:].rearrange("p j d -> p (j d)"), ALU.mult
                                            ).then_inc(msg_done, 1)

            for n in range(EPILOGUE):
                part = slice(n * EPI, (n + 1) * EPI)
                dve.wait_ge(parts_loaded[n % 2], 16 * TILES * (n // 2 + 1))
                for j in range(TILES):
                    add = nc.vector.tensor_tensor(h[:, part], h[:, part], parts[n % 2][:, j], ALU.add)
                    if j == TILES - 1:
                        then_next(add)
                        nc.vector.engine_nop().then_inc(parts_used, 1)
                    else:
                        then_next(add)
                normalise(part, h[:, part], n + 1)
                then_next(nc.vector.tensor_tensor(work[:, part], work[:, part], wide(stat[:, 0, part], EPI), ALU.mult))
                then_next(nc.vector.tensor_tensor(work[:, part], work[:, part],
                                                  gamma.rearrange("p (o d) -> p o d", o=1)
                                                  .to_broadcast([P, EPI, D]), ALU.mult))
                nc.vector.tensor_tensor(work[:, part], work[:, part], x[:, part], ALU.add).then_inc(out_ready, 1)


def kernel(**inputs):
    import numpy as np
    import concourse.bacc as bacc
    from concourse.bass_utils import run_bass_kernel_spmd

    def get(name):
        return np.asarray(inputs[name])

    f32 = np.float32
    x = np.zeros((ROWS, D), f32)
    x[:NODES] = get("x")
    attr = np.zeros((UNITS * UNIT, D), f32)
    attr[:EDGES] = get("edge_attr_64")
    attr = np.ascontiguousarray(attr.reshape(UNITS, 2, HALF, D).transpose(0, 1, 3, 2)).reshape(UNITS, P, HALF)

    def by_tile(ids, fill):
        padded = fill.astype(np.int32)
        padded[:EDGES] = ids
        return padded.reshape(UNITS, 2, CHUNKS, P).transpose(0, 3, 2, 1).reshape(UNITS, P, TILES)

    places = np.arange(UNITS * UNIT)
    index = np.ascontiguousarray(np.concatenate(
        [by_tile(get("src"), NODES + places % P), by_tile(get("dst"), np.full_like(places, NODES - 1))], axis=2))

    const = np.zeros((P, CONST_COLS), f32)
    const[:, C_IDENT:C_IDENT + P] = np.eye(P)
    const[:, C_MASK:C_MASK + P] = np.triu(np.ones((P, P)))
    const[:, C_SPARE] = NODES + np.arange(P)

    value = np.zeros((P, VALUE_COLS), f32)
    for at, name in ((V_W1, "L0_gnn_Wf1"), (V_W2, "L0_gnn_Wf2"), (V_WL, "L0_gnn_Wl")):
        value[:D, at:at + D] = get(name).T
        value[D:, at + D:at + P] = get(name).T
    value[:, V_GAMMA:V_GAMMA + D] = get("L0_gnn_gamma")
    value[:, V_BETA:V_BETA + D] = get("L0_gnn_beta")
    value[:D, V_B1] = get("L0_gnn_bf1")
    value[D:, V_B1] = get("L0_gnn_bf1")

    row = np.zeros((1, ROW_COLS), f32)
    row[0, R_B2:R_B2 + TILES * D] = np.tile(get("L0_gnn_bf2"), TILES)
    row[0, R_BL:R_BL + TILES * D] = np.tile(get("L0_gnn_bl"), TILES)
    row[0, R_ONES:] = 1.0

    nc = bacc.Bacc("TRN2", target_bir_lowering=False, num_devices=1)
    arrays = {"x_in": x, "attr_in": attr, "index_in": index, "const_in": const, "value_in": value, "row_in": row}
    args = [nc.dram_tensor(name, a.shape, mybir.dt.from_np(a.dtype), kind="ExternalInput").ap()
            for name, a in arrays.items()]
    out = nc.dram_tensor("out_rows", (ROWS, D), F32, kind="ExternalOutput").ap()
    build(nc, *args, out)
    result = run_bass_kernel_spmd(nc, [arrays], core_ids=[0])
    return result.results[0]["out_rows"][:NODES]
```

```python
from contextlib import ExitStack

import concourse.bass as bass
from concourse import mybir

ALU = mybir.AluOpType
ACT = mybir.ActivationFunctionType
AX_X = mybir.AxisListType.X
F32 = mybir.dt.float32
I32 = mybir.dt.int32
BF16 = mybir.dt.bfloat16
U32 = mybir.dt.uint32

P = 128
D = 64
NODES = 6250
EDGES = 200000
TILES = 8
UNIT = TILES * P
HALF = UNIT // 2
CHUNKS = TILES // 2
UNITS = 2 * (-(-EDGES // (2 * UNIT)))
BLOCKS = UNITS // 2
W = -(-(NODES + P) // P)
W += W % 2
ROWS = W * P
EPS = 1e-5
EPI = 10

PARTS = 2 * 2 * TILES
C_IDENT, C_MASK, C_PICK, C_SPARE, C_PLACE, C_THIRD = 0, P, 2 * P, (2 + 2 * TILES) * P, (2 + 2 * TILES) * P + 1, (2 + 2 * TILES) * P + 2
CONST_COLS = C_THIRD + 3
V_W1, V_W2, V_WL, V_GAMMA, V_BETA, V_B1 = 0, P, 2 * P, 3 * P, 3 * P + D, 3 * P + 2 * D
VALUE_COLS = V_B1 + 1
THIRDS = 3
R_B2, R_BL, R_ONES = 0, TILES * D, 2 * TILES * D
ROW_COLS = R_ONES + P


def build(nc, x_in, attr_in, index_in, rows_in, dst_in, bits_in, const_in, value_in, row_in, out):
    with ExitStack() as ctx:
        def sb(name, shape, dt=F32):
            return ctx.enter_context(nc.sbuf_tensor(name, shape, dt))

        def psum(name, cols=512):
            return ctx.enter_context(nc.psum_tensor(name, [P, cols], F32))

        def sem(name):
            return ctx.enter_context(nc.semaphore(name))

        def pair(make):
            return [make(u) for u in range(2)]

        wxh_dram = nc.dram_tensor("wxh_rows", (ROWS, D), F32, kind="Internal").ap()
        sums_dram = [nc.dram_tensor(f"sums{j}", (ROWS, D), F32, kind="Internal").ap() for j in range(TILES)]

        x = sb("x", [P, W, D])
        h = sb("h", [P, W, D])
        work = sb("work", [P, W, D])
        square = sb("square", [P, W, D])
        stat = sb("stat", [P, 4, W])
        hT = pair(lambda u: sb(f"hT{u}", [P, 512]))
        const = sb("const", [P, CONST_COLS])
        value = sb("value", [P, VALUE_COLS])
        row = sb("row", [THIRDS, ROW_COLS])
        bits = sb("bits", [PARTS, 1], I32)
        pick = sb("pick", [PARTS, 2 * TILES, P], BF16)
        ones16 = sb("ones16", [THIRDS, P], BF16)
        b2_part = sb("b2_part", [THIRDS, TILES * D], BF16)
        b2_rest = sb("b2_rest", [THIRDS, TILES * D])
        b2_sum = sb("b2_sum", [THIRDS, TILES * D])
        b2_thirds = sb("b2_thirds", [THIRDS, TILES * D], BF16)
        dst_units = sb("dst_units", [BLOCKS, 2, UNIT], I32)
        dst_first = sb("dst_first", [BLOCKS, 2])
        dst_span = sb("dst_span", [BLOCKS, 3, 2])
        dst_far = sb("dst_far", [BLOCKS, 1])
        scattered = sb("scattered", [1, 1], I32)
        window_rows = sb("window_rows", [P, 2, BLOCKS])
        eps = sb("eps", [P, 1])
        attr = pair(lambda u: sb(f"attr{u}", [P, HALF]))
        index = pair(lambda u: sb(f"index{u}", [P, 2 * TILES], I32))
        rows = pair(lambda u: sb(f"rows{u}", [PARTS, P], I32))
        rows_split = pair(lambda u: sb(f"rows_split{u}", [PARTS, P], I32))
        rows16 = pair(lambda u: sb(f"rows16_{u}", [PARTS, P], BF16))
        window = pair(lambda u: sb(f"window{u}", [P, D]))
        onehot = pair(lambda u: sb(f"onehot{u}", [P, TILES, P]))
        src = pair(lambda u: sb(f"src{u}", [P, TILES]))
        hidden = pair(lambda u: sb(f"hidden{u}", [P, HALF]))
        gathered = pair(lambda u: sb(f"gathered{u}", [P, TILES, D]))
        msg = pair(lambda u: sb(f"msg{u}", [P, TILES, D]))
        last_match = pair(lambda u: sb(f"last_match{u}", [P, TILES, P]))
        matches = pair(lambda u: sb(f"matches{u}", [P, TILES]))
        spare = pair(lambda u: sb(f"spare{u}", [P, TILES]))
        target = pair(lambda u: sb(f"target{u}", [P, TILES], U32))
        summed = pair(lambda u: sb(f"summed{u}", [P, TILES, D]))
        parts = pair(lambda u: sb(f"parts{u}", [P, TILES, EPI, D]))

        ps_hidden = psum("ps_hidden")
        ps_filter = psum("ps_filter")
        ps_sum = psum("ps_sum")
        ps_gather = psum("ps_gather")
        ps_src = pair(lambda s: psum(f"ps_src{s}"))
        ps_dst = pair(lambda s: psum(f"ps_dst{s}"))

        ident = const[:, C_IDENT:C_IDENT + P]
        mask = const[:, C_MASK:C_MASK + P]
        pick_in = const[0:PARTS, C_PICK:C_PICK + 2 * TILES * P].rearrange("k (j p) -> k j p", p=P)
        spare_row = const[:, C_SPARE:C_SPARE + 1]
        place = const[:, C_PLACE:C_PLACE + 1]
        w1 = value[:, V_W1:V_W1 + P]
        w2 = value[:, V_W2:V_W2 + P]
        wl = value[:, V_WL:V_WL + P]
        gamma = value[:, V_GAMMA:V_GAMMA + D]
        beta = value[:, V_BETA:V_BETA + D]
        b1 = value[:, V_B1:V_B1 + 1]
        b2 = row[:, R_B2:R_B2 + TILES * D]
        bl = row[0:1, R_BL:R_BL + TILES * D]
        ones = row[0:1, R_ONES:R_ONES + P]

        x_loaded = sem("x_loaded")
        const_loaded = sem("const_loaded")
        zeros_ready = sem("zeros_ready")
        eps_ready = sem("eps_ready")
        ln_step = sem("ln_step")
        centred = sem("centred")
        squared = sem("squared")
        variance = sem("variance")
        deviation = sem("deviation")
        h_ready = sem("h_ready")
        h_turned = sem("h_turned")
        hT_ready = sem("hT_ready")
        wxh_done = sem("wxh_done")
        wxh_copied = sem("wxh_copied")
        wxh_stored = sem("wxh_stored")
        dst_loaded = sem("dst_loaded")
        cast_done = sem("cast_done")
        first_ready = sem("first_ready")
        first_spread = sem("first_spread")
        far_ready = sem("far_ready")
        far_turned = sem("far_turned")
        way_ready = sem("way_ready")
        rows_loaded = pair(lambda u: sem(f"rows_loaded{u}"))
        split_done = pair(lambda u: sem(f"split_done{u}"))
        rows_ready = pair(lambda u: sem(f"rows_ready{u}"))
        window_loaded = pair(lambda u: sem(f"window_loaded{u}"))
        dst_spread = pair(lambda s: sem(f"dst_spread{s}"))
        onehot_built = pair(lambda s: sem(f"onehot_built{s}"))
        picked = pair(lambda u: sem(f"picked{u}"))
        picked_copied = pair(lambda u: sem(f"picked_copied{u}"))
        attr_loaded = pair(lambda u: sem(f"attr_loaded{u}"))
        index_loaded = pair(lambda u: sem(f"index_loaded{u}"))
        mlp1_done = pair(lambda u: sem(f"mlp1_done{u}"))
        silu_done = pair(lambda u: sem(f"silu_done{u}"))
        src_ready = pair(lambda u: sem(f"src_ready{u}"))
        src_spread = pair(lambda s: sem(f"src_spread{s}"))
        match_built = pair(lambda s: sem(f"match_built{s}"))
        spare_done = sem("spare_done")
        target_ready = pair(lambda u: sem(f"target_ready{u}"))
        filter_done = pair(lambda u: sem(f"filter_done{u}"))
        gather_done = pair(lambda u: sem(f"gather_done{u}"))
        load_go = sem("load_go")
        window_go = sem("window_go")
        gather_go = sem("gather_go")
        scatter_go = sem("scatter_go")
        msg_done = sem("msg_done")
        sum_done = pair(lambda u: sem(f"sum_done{u}"))
        sum_copied = sem("sum_copied")
        settled = [sem(f"settled{j}") for j in range(TILES)]
        parts_loaded = pair(lambda u: sem(f"parts_loaded{u}"))
        parts_used = sem("parts_used")
        out_ready = sem("out_ready")
        out_stored = sem("out_stored")

        def node_rows(t):
            return t.rearrange("(p w) d -> p w d", p=P)

        BATCHES = [(w0, min(w0 + 8, W)) for w0 in range(0, W, 8)]
        EPILOGUE = W // EPI

        def choose(eng, edges):
            eng.wait_ge(way_ready, 1)
            indirect = eng.value_load(scattered[0:1, 0:1], min_val=0, max_val=1)
            with eng.If(indirect == 0):
                edges(True)
            with eng.Else():
                edges(False)

        block = ctx.enter_context(nc.Block())

        @block.sync
        def _(sp):
            sp.dma_start(x[:], node_rows(x_in)).then_inc(x_loaded, 16)
            sp.dma_start(const[:], const_in).then_inc(const_loaded, 16)
            sp.dma_start(value[:], value_in).then_inc(const_loaded, 16)
            sp.dma_start(row[:], row_in).then_inc(const_loaded, 16)

            sp.dma_start(bits[:], bits_in).then_inc(const_loaded, 16)

            def load(g, u):
                sp.dma_start(index[u][:], index_in[g]).then_inc(index_loaded[u], 16)
                sp.dma_start(rows[u][:], rows_in[g]).then_inc(rows_loaded[u], 16)
                sp.dma_start(attr[u][:], attr_in[g]).then_inc(attr_loaded[u], 16)

            def buffers_free(u, n, windowed):
                if not windowed:
                    sp.wait_ge(gather_done[u], 16 * TILES * n)
                sp.wait_ge(src_ready[u], n)
                sp.wait_ge(split_done[u], n)
                sp.wait_ge(mlp1_done[u], n)
                sp.sem_inc(load_go, 1)

            def load_window(u, n):
                sp.wait_ge(index_loaded[u], 16 * (n + 1))
                sp.wait_ge(picked[u], n)
                sp.sem_inc(window_go, 1)
                first = sp.value_load(index[u][0:1, TILES:TILES + 1], min_val=0, max_val=NODES - 1)
                sp.dma_start(window[u][:], wxh_dram[bass.ds(first, P), :]).then_inc(window_loaded[u], 16)

            sp.dma_start(dst_units[:], dst_in).then_inc(dst_loaded, 16)
            load(0, 0)
            load(1, 1)
            sp.wait_ge(wxh_copied, len(BATCHES))
            sp.dma_start(node_rows(wxh_dram), work[:]).then_inc(wxh_stored, 16)
            sp.wait_ge(wxh_stored, 16)

            def edges(windowed):
                if windowed:
                    load_window(0, 0)
                    load_window(1, 0)
                with sp.Fori(0, BLOCKS - 1) as b:
                    for u in range(2):
                        buffers_free(u, b + 1, windowed)
                        load(2 * b + 2 + u, u)
                        if windowed:
                            load_window(u, b + 1)

            choose(sp, edges)

            for j in range(TILES):
                sp.wait_ge(settled[j], 16 * (UNITS + 1))
            for n in range(EPILOGUE):
                if n >= 2:
                    sp.wait_ge(parts_used, n - 1)
                for j in range(TILES):
                    sp.dma_start(parts[n % 2][:, j], node_rows(sums_dram[j])[:, n * EPI:(n + 1) * EPI]
                                 ).then_inc(parts_loaded[n % 2], 16)
            sp.wait_ge(out_ready, EPILOGUE)
            sp.dma_start(node_rows(out), work[:]).then_inc(out_stored, 16)
            sp.wait_ge(out_stored, 16)

        @block.gpsimd
        def _(pool):
            nc.gpsimd.memset(eps[:], EPS).then_inc(eps_ready, 1)
            nc.gpsimd.memset(square[:], 0.0).then_inc(zeros_ready, 1)
            pool.wait_ge(zeros_ready, 1)
            for j in range(TILES):
                pool.dma_start(node_rows(sums_dram[j]), square[:]).then_inc(settled[j], 16)

            def gather(u, n):
                pool.wait_ge(index_loaded[u], 16 * n)
                pool.wait_ge(sum_done[u], n - 1)
                pool.sem_inc(gather_go, 1)
                for j in range(TILES):
                    pool.indirect_dma_start(
                        gathered[u][:, j], None, wxh_dram,
                        bass.IndirectOffsetOnAxis(ap=index[u][:, TILES + j:TILES + j + 1].bitcast(U32), axis=0),
                    ).then_inc(gather_done[u], 16)

            def scatter(u, n, g):
                pool.wait_ge(target_ready[u], n)
                pool.wait_ge(sum_copied, g + 1)
                for j in range(TILES):
                    pool.wait_ge(settled[j], 16 * (g + 1))
                    pool.sem_inc(scatter_go, 1)
                    pool.indirect_dma_start(
                        sums_dram[j], bass.IndirectOffsetOnAxis(ap=target[u][:, j:j + 1], axis=0),
                        summed[u][:, j], None, compute_op=ALU.add).then_inc(settled[j], 16)

            pool.wait_ge(wxh_stored, 16)

            def edges(windowed):
                if not windowed:
                    gather(0, 1)
                with pool.Fori(0, BLOCKS - 1) as b:
                    if not windowed:
                        gather(1, b + 1)
                    scatter(0, b + 1, 2 * b)
                    if not windowed:
                        gather(0, b + 2)
                    scatter(1, b + 1, 2 * b + 1)
                if not windowed:
                    gather(1, BLOCKS)
                scatter(0, BLOCKS, UNITS - 2)
                scatter(1, BLOCKS, UNITS - 1)

            choose(pool, edges)

        def project(pe, n):
            w0, w1_ = BATCHES[n]
            cols = (w1_ - w0) * D
            acc = [ps_hidden, ps_filter][n % 2]
            pe.wait_ge(hT_ready, n + 1)
            if n >= 2:
                pe.wait_ge(wxh_copied, n - 1)
            nc.tensor.matmul(acc[:, :cols], ones, bl[:, :cols], start=True, stop=False)
            for k in range(cols // P):
                last = nc.tensor.matmul(acc[:, k * P:(k + 1) * P], hT[n % 2][:, k * P:(k + 1) * P], wl,
                                        start=False, stop=(k == cols // P - 1))
            last.then_inc(wxh_done, 1)

        def enter_unit(pe, u, b, windowed):
            g = 2 * b + u
            pe.wait_ge(rows_ready[u], b + 1)
            for s in range(2):
                if windowed:
                    pe.wait_ge(onehot_built[s], g)
                    for k in range(4):
                        last = nc.tensor.matmul(ps_dst[s][:, k * P:(k + 1) * P], pick[:, TILES + 4 * s + k, :],
                                                rows16[u][:], start=True, stop=True)
                    last.then_inc(dst_spread[s], 1)
            pe.wait_ge(attr_loaded[u], 16 * (b + 1))
            pe.wait_ge(silu_done[1 - u], b + u)
            nc.tensor.matmul(ps_hidden[:], w1, attr[u][:], start=True, stop=True).then_inc(mlp1_done[u], 1)
            for s in range(2):
                pe.wait_ge(match_built[s], g)
                for k in range(4):
                    last = nc.tensor.matmul(ps_src[s][:, k * P:(k + 1) * P], pick[:, 4 * s + k, :],
                                            rows16[u][:], start=True, stop=True)
                last.then_inc(src_spread[s], 1)

        def middle_of_unit(pe, u, b, windowed):
            g = 2 * b + u
            if windowed:
                pe.wait_ge(picked_copied[1 - u], b + u)
                pe.wait_ge(window_loaded[u], 16 * (b + 1))
                for s in range(2):
                    pe.wait_ge(onehot_built[s], g + 1)
                    for j in range(4 * s, 4 * s + 4):
                        last = nc.tensor.matmul(ps_gather[:, j * D:(j + 1) * D], onehot[u][:, j], window[u][:],
                                                start=True, stop=True)
                last.then_inc(picked[u], 1)
            pe.wait_ge(msg_done, g)
            nc.tensor.matmul(ps_filter[:], ones16[:], b2_thirds[:], start=True, stop=False)
            pe.wait_ge(silu_done[u], b + 1)
            for k in range(CHUNKS):
                last = nc.tensor.matmul(ps_filter[:, k * P:(k + 1) * P], hidden[u][:, k * P:(k + 1) * P], w2,
                                        start=False, stop=(k == CHUNKS - 1))
            last.then_inc(filter_done[u], 1)

        def leave_unit(pe, u, b):
            g = 2 * b + u
            pe.wait_ge(sum_copied, g)
            pe.wait_ge(msg_done, g + 1)
            pe.wait_ge(match_built[0], g + 1)
            pe.wait_ge(match_built[1], g + 1)
            for j in range(TILES):
                last = nc.tensor.matmul(ps_sum[:, j * D:(j + 1) * D], last_match[u][:, j], msg[u][:, j],
                                        start=True, stop=True)
            last.then_inc(sum_done[u], 1)

        @block.tensor
        def _(pe):
            pe.wait_ge(const_loaded, 64)
            pe.wait_ge(first_ready, 1)
            for u in range(2):
                last = nc.tensor.transpose(ps_dst[0][:, u * BLOCKS:(u + 1) * BLOCKS],
                                           dst_first[:, u:u + 1].to_broadcast([BLOCKS, P]),
                                           ident[0:BLOCKS, 0:BLOCKS])
            last.then_inc(first_spread, 1)
            pe.wait_ge(far_ready, 1)
            nc.tensor.transpose(ps_dst[1][0:1, 0:BLOCKS], dst_far[:], ident[0:BLOCKS, 0:BLOCKS]).then_inc(far_turned, 1)
            pe.wait_ge(h_ready, 1)
            for n, (w0, w1_) in enumerate(BATCHES):
                if n >= 2:
                    pe.wait_ge(hT_ready, n - 1)
                for k in range((w1_ - w0) // 2):
                    last = nc.tensor.transpose([ps_src[0], ps_src[1]][n % 2][:, k * P:(k + 1) * P],
                                               h[:, w0 + 2 * k:w0 + 2 * k + 2, :].rearrange("p w d -> p (w d)"),
                                               ident)
                last.then_inc(h_turned, 1)
                if n >= 1:
                    project(pe, n - 1)
            project(pe, len(BATCHES) - 1)

            pe.wait_ge(cast_done, 4)
            pe.wait_ge(wxh_copied, len(BATCHES))
            pe.wait_ge(way_ready, 1)

            def edges(windowed):
                enter_unit(pe, 0, 0, windowed)
                with pe.Fori(0, BLOCKS - 1) as b:
                    for u in range(2):
                        middle_of_unit(pe, u, b, windowed)
                        enter_unit(pe, 1 - u, b + u, windowed)
                        leave_unit(pe, u, b)
                middle_of_unit(pe, 0, BLOCKS - 1, windowed)
                enter_unit(pe, 1, BLOCKS - 1, windowed)
                leave_unit(pe, 0, BLOCKS - 1)
                middle_of_unit(pe, 1, BLOCKS - 1, windowed)
                leave_unit(pe, 1, BLOCKS - 1)

            choose(pe, edges)

        @block.scalar
        def _(act):
            act.wait_ge(centred, 1)
            act.wait_ge(settled[0], 16)
            for j in range(1, TILES):
                act.wait_ge(settled[j], 16)
            nc.scalar.activation(square[:], work[:], ACT.Square).then_inc(squared, 1)
            act.wait_ge(variance, 1)
            act.wait_ge(eps_ready, 1)
            nc.scalar.activation(stat[:, 3], stat[:, 2], ACT.Sqrt, bias=eps[:], scale=1.0 / D).then_inc(deviation, 1)
            for n, (w0, w1_) in enumerate(BATCHES):
                act.wait_ge(wxh_done, n + 1)
                nc.scalar.copy(work[:, w0:w1_, :].rearrange("p w d -> p (w d)"),
                               [ps_hidden, ps_filter][n % 2][:, :(w1_ - w0) * D]).then_inc(wxh_copied, 1)

            def edges(windowed):
                with act.Fori(0, BLOCKS) as b:
                    for u in range(2):
                        g = 2 * b + u
                        act.wait_ge(mlp1_done[u], b + 1)
                        act.wait_ge(filter_done[u], b)
                        nc.scalar.activation(hidden[u][:], ps_hidden[:], ACT.Silu, bias=b1).then_inc(silu_done[u], 1)
                        if windowed:
                            act.wait_ge(picked[u], b + 1)
                            act.wait_ge(sum_done[u], b)
                            nc.scalar.copy(gathered[u][:].rearrange("p j d -> p (j d)"), ps_gather[:]
                                           ).then_inc(picked_copied[u], 1)
                        act.wait_ge(sum_done[u], b + 1)
                        for j in range(TILES):
                            act.wait_ge(settled[j], 16 * g)
                        nc.scalar.copy(summed[u][:].rearrange("p j d -> p (j d)"), ps_sum[:]).then_inc(sum_copied, 1)

            choose(act, edges)
            for n in range(EPILOGUE):
                part = slice(n * EPI, (n + 1) * EPI)
                act.wait_ge(centred, n + 2)
                nc.scalar.activation(square[:, part], work[:, part], ACT.Square).then_inc(squared, 1)
                act.wait_ge(variance, n + 2)
                nc.scalar.activation(stat[:, 3, part], stat[:, 2, part], ACT.Sqrt, bias=eps[:],
                                     scale=1.0 / D).then_inc(deviation, 1)

        @block.vector
        def _(dve):
            steps = [0]

            def then_next(ins):
                steps[0] += 1
                ins.then_inc(ln_step, 1)
                dve.wait_ge(ln_step, steps[0])

            def wide(column, n):
                return column.rearrange("p (w o) -> p w o", o=1).to_broadcast([P, n, D])

            def normalise(part, y, n):
                cols = part.stop - part.start
                then_next(nc.vector.tensor_reduce(stat[:, 0, part], y, AX_X, ALU.add))
                then_next(nc.vector.tensor_scalar(stat[:, 1, part], stat[:, 0, part], -1.0 / D, None, ALU.mult))
                nc.vector.tensor_tensor(work[:, part], y, wide(stat[:, 1, part], cols), ALU.add).then_inc(centred, 1)
                dve.wait_ge(squared, n + 1)
                nc.vector.tensor_reduce(stat[:, 2, part], square[:, part], AX_X, ALU.add).then_inc(variance, 1)
                dve.wait_ge(deviation, n + 1)
                then_next(nc.vector.reciprocal(stat[:, 0, part], stat[:, 3, part]))

            def way():
                dve.wait_ge(dst_loaded, 16)
                then_next(nc.vector.tensor_copy(dst_first[:], dst_units[:, :, 0]))
                nc.vector.engine_nop().then_inc(first_ready, 1)
                first, low, high = dst_first[:], dst_span[:, 0, :], dst_span[:, 1, :]
                then_next(nc.vector.tensor_reduce(low, dst_units[:], AX_X, ALU.min))
                then_next(nc.vector.tensor_reduce(high, dst_units[:], AX_X, ALU.max))
                then_next(nc.vector.tensor_tensor(low, first, low, ALU.subtract))
                then_next(nc.vector.scalar_tensor_tensor(out=high, in0=high, scalar=1.0 - P, in1=first,
                                                         op0=ALU.add, op1=ALU.subtract))
                then_next(nc.vector.tensor_tensor(dst_span[:, 2, :], low, high, ALU.max))
                nc.vector.tensor_reduce(dst_far[:], dst_span[:, 2, :], AX_X, ALU.max).then_inc(far_ready, 1)
                dve.wait_ge(first_spread, 1)
                nc.vector.tensor_scalar(window_rows[:].rearrange("p u b -> p (u b)"), ps_dst[0][:, 0:2 * BLOCKS],
                                        place, None, ALU.add).then_inc(cast_done, 1)
                dve.wait_ge(far_turned, 1)
                then_next(nc.vector.tensor_reduce(dst_first[0:1, 0:1], ps_dst[1][0:1, 0:BLOCKS], AX_X, ALU.max))
                nc.vector.tensor_scalar(scattered[:], dst_first[0:1, 0:1], 0.0, None, ALU.is_gt
                                        ).then_inc(way_ready, 1)

            def constants():
                nc.vector.tensor_copy(pick[:], pick_in).then_inc(cast_done, 1)
                nc.vector.memset(ones16[:], 1.0).then_inc(cast_done, 1)
                third = [const[0:THIRDS, C_THIRD + n:C_THIRD + n + 1] for n in range(THIRDS)]
                rest = b2
                for n in range(THIRDS - 1):
                    then_next(nc.vector.tensor_copy(b2_part[:], rest))
                    then_next(nc.vector.tensor_tensor(b2_rest[:], rest, b2_part[:], ALU.subtract))
                    if n == 0:
                        then_next(nc.vector.tensor_scalar(b2_sum[:], b2_part[:], third[0], None, ALU.mult))
                    else:
                        then_next(nc.vector.scalar_tensor_tensor(out=b2_sum[:], in0=b2_part[:], scalar=third[n],
                                                                 in1=b2_sum[:], op0=ALU.mult, op1=ALU.add))
                    rest = b2_rest[:]
                nc.vector.scalar_tensor_tensor(out=b2_thirds[:], in0=rest, scalar=third[THIRDS - 1], in1=b2_sum[:],
                                               op0=ALU.mult, op1=ALU.add).then_inc(cast_done, 1)

            dve.wait_ge(x_loaded, 16)
            whole = slice(0, W)
            normalise(whole, x[:], 0)
            nc.vector.scalar_tensor_tensor(out=h[:], in0=work[:], scalar=0.0, in1=wide(stat[:, 0, whole], W),
                                           op0=ALU.max, op1=ALU.mult).then_inc(h_ready, 1)
            way()
            dve.wait_ge(const_loaded, 64)
            constants()
            then_next(nc.vector.tensor_tensor(x[:], x[:], beta.rearrange("p (o d) -> p o d", o=1)
                                              .to_broadcast([P, W, D]), ALU.add))
            for n, (w0, w1_) in enumerate(BATCHES):
                cols = (w1_ - w0) * D
                dve.wait_ge(h_turned, n + 1)
                if n >= 2:
                    dve.wait_ge(wxh_done, n - 1)
                nc.vector.tensor_copy(hT[n % 2][:, :cols], ps_src[n % 2][:, :cols]).then_inc(hT_ready, 1)


            def split_rows(u, n):
                dve.wait_ge(rows_loaded[u], 16 * n)
                nc.vector.tensor_scalar(rows_split[u][:], rows[u][:], bits[:], None, ALU.bitwise_and
                                        ).then_inc(split_done[u], 1)
                dve.wait_ge(split_done[u], n)
                nc.vector.tensor_copy(rows16[u][:], rows_split[u][:]).then_inc(rows_ready[u], 1)

            def edge_unit(u, b, windowed, ahead):
                g = 2 * b + u
                dve.wait_ge(index_loaded[u], 16 * (b + 1))
                nc.vector.tensor_copy(src[u][:], index[u][:, 0:TILES]).then_inc(src_ready[u], 1)
                if windowed:
                    dve.wait_ge(picked[u], b)
                    for s in range(2):
                        dve.wait_ge(dst_spread[s], g + 1)
                        nc.vector.tensor_scalar(
                            onehot[u][:, 4 * s:4 * s + 4, :].rearrange("p j e -> p (j e)"), ps_dst[s][:],
                            window_rows[:, u, bass.ds(b, 1)], None, ALU.is_equal).then_inc(onehot_built[s], 1)
                if ahead:
                    split_rows(1 - u, b + 1 + u)
                dve.wait_ge(src_ready[u], b + 1)
                dve.wait_ge(sum_done[u], b)
                for s in range(2):
                    dve.wait_ge(src_spread[s], g + 1)
                    for k in range(4):
                        j = 4 * s + k
                        last = nc.vector.scalar_tensor_tensor(
                            out=last_match[u][:, j], in0=ps_src[s][:, k * P:(k + 1) * P],
                            scalar=src[u][:, j:j + 1], in1=mask, op0=ALU.is_equal, op1=ALU.mult,
                            accum_out=matches[u][:, j:j + 1])
                    last.then_inc(match_built[s], 1)
                dve.wait_ge(filter_done[u], b + 1)
                if windowed:
                    dve.wait_ge(picked_copied[u], b + 1)
                else:
                    dve.wait_ge(gather_done[u], 16 * TILES * (b + 1))
                nc.vector.tensor_tensor(msg[u][:].rearrange("p j d -> p (j d)"), ps_filter[:],
                                        gathered[u][:].rearrange("p j d -> p (j d)"), ALU.mult
                                        ).then_inc(msg_done, 1)
                dve.wait_ge(match_built[0], g + 1)
                dve.wait_ge(match_built[1], g + 1)
                nc.vector.tensor_scalar(spare[u][:], matches[u][:], 1.0, spare_row, ALU.is_gt,
                                        ALU.mult).then_inc(spare_done, 1)
                dve.wait_ge(spare_done, g + 1)
                for j in range(TILES):
                    dve.wait_ge(settled[j], 16 * g)
                nc.vector.tensor_tensor(target[u][:], spare[u][:], src[u][:], ALU.max
                                        ).then_inc(target_ready[u], 1)

            def edges(windowed):
                split_rows(0, 1)
                with dve.Fori(0, BLOCKS - 1) as b:
                    for u in range(2):
                        edge_unit(u, b, windowed, ahead=True)
                edge_unit(0, BLOCKS - 1, windowed, ahead=True)
                edge_unit(1, BLOCKS - 1, windowed, ahead=False)

            choose(dve, edges)

            for n in range(EPILOGUE):
                part = slice(n * EPI, (n + 1) * EPI)
                dve.wait_ge(parts_loaded[n % 2], 16 * TILES * (n // 2 + 1))
                for j in range(TILES):
                    add = nc.vector.tensor_tensor(h[:, part], h[:, part], parts[n % 2][:, j], ALU.add)
                    if j == TILES - 1:
                        then_next(add)
                        nc.vector.engine_nop().then_inc(parts_used, 1)
                    else:
                        then_next(add)
                normalise(part, h[:, part], n + 1)
                then_next(nc.vector.tensor_tensor(work[:, part], work[:, part], wide(stat[:, 0, part], EPI), ALU.mult))
                then_next(nc.vector.tensor_tensor(work[:, part], work[:, part],
                                                  gamma.rearrange("p (o d) -> p o d", o=1)
                                                  .to_broadcast([P, EPI, D]), ALU.mult))
                nc.vector.tensor_tensor(work[:, part], work[:, part], x[:, part], ALU.add).then_inc(out_ready, 1)


def kernel(**inputs):
    import numpy as np
    import concourse.bacc as bacc
    from concourse.bass_utils import run_bass_kernel_spmd

    def get(name):
        return np.asarray(inputs[name])

    f32 = np.float32
    x = np.zeros((ROWS, D), f32)
    x[:NODES] = get("x")
    attr = np.zeros((UNITS * UNIT, D), f32)
    attr[:EDGES] = get("edge_attr_64")
    attr = np.ascontiguousarray(attr.reshape(UNITS, 2, HALF, D).transpose(0, 1, 3, 2)).reshape(UNITS, P, HALF)

    def by_tile(ids, fill):
        padded = fill.astype(np.int32)
        padded[:EDGES] = ids
        return padded.reshape(UNITS, 2, CHUNKS, P).transpose(0, 3, 2, 1).reshape(UNITS, P, TILES)

    places = np.arange(UNITS * UNIT)
    index = np.ascontiguousarray(np.concatenate(
        [by_tile(get("src"), NODES + places % P), by_tile(get("dst"), np.full_like(places, NODES - 1))], axis=2))

    rows = index.transpose(0, 2, 1)
    rows = np.ascontiguousarray(np.concatenate([rows, rows], axis=1))
    bits = np.repeat(np.array([-P, P - 1], np.int32), PARTS // 2).reshape(PARTS, 1)
    dst_units = np.full((BLOCKS, 2, UNIT), NODES - 1, np.int32)
    dst_units.reshape(-1)[:EDGES] = get("dst")

    const = np.zeros((P, CONST_COLS), f32)
    const[:, C_PLACE] = np.arange(P)
    for j in range(2 * TILES):
        const[[j, j + PARTS // 2], C_PICK + j * P:C_PICK + (j + 1) * P] = 1.0
    const[:THIRDS, C_THIRD:C_THIRD + THIRDS] = np.eye(THIRDS)
    const[:, C_IDENT:C_IDENT + P] = np.eye(P)
    const[:, C_MASK:C_MASK + P] = np.triu(np.ones((P, P)))
    const[:, C_SPARE] = NODES + np.arange(P)

    value = np.zeros((P, VALUE_COLS), f32)
    for at, name in ((V_W1, "L0_gnn_Wf1"), (V_W2, "L0_gnn_Wf2"), (V_WL, "L0_gnn_Wl")):
        value[:D, at:at + D] = get(name).T
        value[D:, at + D:at + P] = get(name).T
    value[:, V_GAMMA:V_GAMMA + D] = get("L0_gnn_gamma")
    value[:, V_BETA:V_BETA + D] = get("L0_gnn_beta")
    value[:D, V_B1] = get("L0_gnn_bf1")
    value[D:, V_B1] = get("L0_gnn_bf1")

    row = np.zeros((THIRDS, ROW_COLS), f32)
    row[:, R_B2:R_B2 + TILES * D] = np.tile(get("L0_gnn_bf2"), TILES)
    row[:, R_BL:R_BL + TILES * D] = np.tile(get("L0_gnn_bl"), TILES)
    row[:, R_ONES:] = 1.0

    nc = bacc.Bacc("TRN2", target_bir_lowering=False, num_devices=1)
    arrays = {"x_in": x, "attr_in": attr, "index_in": index, "rows_in": rows,
              "dst_in": dst_units, "bits_in": bits, "const_in": const, "value_in": value, "row_in": row}
    args = [nc.dram_tensor(name, a.shape, mybir.dt.from_np(a.dtype), kind="ExternalInput").ap()
            for name, a in arrays.items()]
    out = nc.dram_tensor("out_rows", (ROWS, D), F32, kind="ExternalOutput").ap()
    build(nc, *args, out)
    result = run_bass_kernel_spmd(nc, [arrays], core_ids=[0])
    return result.results[0]["out_rows"][:NODES]
```

```python
from contextlib import ExitStack

import concourse.bass as bass
from concourse import mybir

ALU = mybir.AluOpType
ACT = mybir.ActivationFunctionType
AX_X = mybir.AxisListType.X
F32 = mybir.dt.float32
I32 = mybir.dt.int32
I16 = mybir.dt.int16
U32 = mybir.dt.uint32

P = 128
D = 64
NODES = 6250
EDGES = 200000
TILES = 8
UNIT = TILES * P
HALF = UNIT // 2
CHUNKS = TILES // 2
QUAD = 4
UNITS = QUAD * (-(-EDGES // (QUAD * UNIT)))
QUADS = UNITS // QUAD
PEELED = 2 * QUAD
BLOCKS = UNITS // 2
FEW = TILES // 2
W = -(-(NODES + P) // P)
W += W % 2
ROWS = W * P
EPS = 1e-5
BATCH = 8

C_IDENT, C_MASK, C_SPARE, C_PLACE = 0, P, 2 * P, 2 * P + 1
CONST_COLS = C_PLACE + 1
V_W1, V_W2, V_WL, V_GAMMA = 0, P, 2 * P, 3 * P
V_BETA, V_BL, V_B2, V_B1 = V_GAMMA + D, V_GAMMA + 2 * D, V_GAMMA + 3 * D, V_GAMMA + 4 * D
VALUE_COLS = V_B1 + 1


def scatters(g):
    held = [j for j in range(TILES) if g * UNIT + (j % 2) * HALF + (j // 2) * P < EDGES]
    few = g < PEELED - 1 or g >= UNITS - QUAD
    return [(j, j % FEW if few else j) for j in held]


def landings(a, g):
    return 16 * sum(to == a for before in range(g) for _, to in scatters(before))


def build(nc, x_in, attr_in, index_in, rows_in, const_in, value_in, out):
    with ExitStack() as ctx:
        def sb(name, shape, dt=F32):
            return ctx.enter_context(nc.sbuf_tensor(name, shape, dt))

        def psum(name, cols=512):
            return ctx.enter_context(nc.psum_tensor(name, [P, cols], F32))

        def sem(name):
            return ctx.enter_context(nc.semaphore(name))

        def pair(make):
            return [make(u) for u in range(2)]

        rows_dram = nc.dram_tensor("id_rows", (UNITS, 2 * TILES * P), I16, kind="Internal").ap()
        wxh_dram = nc.dram_tensor("wxh_rows", (ROWS, D), F32, kind="Internal").ap()
        sums_dram = [nc.dram_tensor(f"sums{j}", (ROWS, D), F32, kind="Internal").ap() for j in range(TILES)]

        x = sb("x", [P, W, D])
        h = sb("h", [P, W, D])
        work = sb("work", [P, W, D])
        square = sb("square", [P, W, D])
        zeros = sb("zeros", [P, W * D])
        stat = sb("stat", [P, 4, W])
        hT = pair(lambda u: sb(f"hT{u}", [P, 512]))
        const = sb("const", [P, CONST_COLS])
        value = sb("value", [P, VALUE_COLS])
        ids = sb("ids", [BLOCKS, 2, 2 * TILES, P], I32)
        ids16 = sb("ids16", [BLOCKS, 2, 2 * TILES, P], I16)
        dst_first = sb("dst_first", [BLOCKS, 2])
        dst_span = sb("dst_span", [BLOCKS, 3, 2])
        dst_far = sb("dst_far", [BLOCKS, 1])
        scattered = sb("scattered", [1, 1], I32)
        window_rows = sb("window_rows", [P, 2, BLOCKS])
        eps = sb("eps", [P, 1])
        silu_first = sb("silu_first", [P, 1])
        attr = pair(lambda u: sb(f"attr{u}", [P, HALF]))
        index = pair(lambda u: sb(f"index{u}", [P, 2 * TILES], I32))
        rows = pair(lambda u: sb(f"rows{u}", [P, 2 * TILES, P], I16))
        window = pair(lambda u: sb(f"window{u}", [P, D]))
        onehot = pair(lambda u: sb(f"onehot{u}", [P, TILES, P]))
        src = pair(lambda u: sb(f"src{u}", [P, TILES]))
        hidden = pair(lambda u: sb(f"hidden{u}", [P, HALF]))
        gathered = pair(lambda u: sb(f"gathered{u}", [P, TILES, D]))
        msg = pair(lambda u: sb(f"msg{u}", [P, TILES, D]))
        last_match = pair(lambda u: sb(f"last_match{u}", [P, TILES, P]))
        matches = pair(lambda u: sb(f"matches{u}", [P, TILES]))
        spare = pair(lambda u: sb(f"spare{u}", [P, TILES]))
        target = [sb(f"target{q}", [P, TILES], U32) for q in range(QUAD)]
        summed = [sb(f"summed{q}", [P, TILES, D]) for q in range(QUAD)]
        parts = pair(lambda u: sb(f"parts{u}", [P, FEW, BATCH, D]))
        more = [square[:], zeros[:].rearrange("p (w d) -> p w d", d=D)]
        more += [sb(f"more{k}", [P, W, D])[:] for k in range(TILES - FEW - len(more))]
        side = pair(lambda u: sb(f"side{u}", [P, BATCH, D]))

        ps_hidden = psum("ps_hidden")
        ps_filter = psum("ps_filter")
        ps_sum = psum("ps_sum")
        ps_gather = psum("ps_gather")
        ps_turn = pair(lambda s: psum(f"ps_turn{s}"))
        ps_first = psum("ps_first")
        ps_far = psum("ps_far")

        ident = const[:, C_IDENT:C_IDENT + P]
        mask = const[:, C_MASK:C_MASK + P]
        spare_row = const[:, C_SPARE:C_SPARE + 1]
        place = const[:, C_PLACE:C_PLACE + 1]
        w1 = value[:, V_W1:V_W1 + P]
        w2 = value[:, V_W2:V_W2 + P]
        wl = value[:, V_WL:V_WL + P]
        gamma = value[:, V_GAMMA:V_GAMMA + D]
        beta = value[:, V_BETA:V_BETA + D]
        b1 = value[:, V_B1:V_B1 + 1]
        bl = value[:, V_BL:V_BL + D]
        b2 = value[:, V_B2:V_B2 + D]

        x_loaded = pair(lambda u: sem(f"x_loaded{u}"))
        const_loaded = sem("const_loaded")
        zeros_ready = sem("zeros_ready")
        eps_ready = sem("eps_ready")
        ln_step = sem("ln_step")
        centred = sem("centred")
        squared = sem("squared")
        variance = sem("variance")
        deviation = sem("deviation")
        h_ready = sem("h_ready")
        h_turned = sem("h_turned")
        hT_ready = sem("hT_ready")
        wxh_done = sem("wxh_done")
        wxh_ready = sem("wxh_ready")
        wxh_stored = sem("wxh_stored")
        ids_loaded = sem("ids_loaded")
        ids16_ready = sem("ids16_ready")
        rows_stored = sem("rows_stored")
        pool_step = sem("pool_step")
        x_beta_done = sem("x_beta_done")
        window_rows_ready = sem("window_rows_ready")
        first_ready = sem("first_ready")
        first_spread = sem("first_spread")
        far_ready = sem("far_ready")
        far_turned = sem("far_turned")
        way_ready = sem("way_ready")
        rows_loaded = pair(lambda u: sem(f"rows_loaded{u}"))
        window_loaded = pair(lambda u: sem(f"window_loaded{u}"))
        onehot_built = pair(lambda u: sem(f"onehot_built{u}"))
        picked = pair(lambda u: sem(f"picked{u}"))
        picked_copied = pair(lambda u: sem(f"picked_copied{u}"))
        attr_loaded = pair(lambda u: sem(f"attr_loaded{u}"))
        index_loaded = pair(lambda u: sem(f"index_loaded{u}"))
        mlp1_done = pair(lambda u: sem(f"mlp1_done{u}"))
        silu_done = pair(lambda u: sem(f"silu_done{u}"))
        src_ready = pair(lambda u: sem(f"src_ready{u}"))
        match_built = pair(lambda u: sem(f"match_built{u}"))
        spare_done = sem("spare_done")
        target_ready = pair(lambda u: sem(f"target_ready{u}"))
        filter_done = pair(lambda u: sem(f"filter_done{u}"))
        gather_done = pair(lambda u: sem(f"gather_done{u}"))
        load_go = sem("load_go")
        window_go = sem("window_go")
        gather_go = sem("gather_go")
        scatter_go = sem("scatter_go")
        filter_read = sem("filter_read")
        msg_done = sem("msg_done")
        sum_done = pair(lambda u: sem(f"sum_done{u}"))
        sum_copied = sem("sum_copied")
        earlier_landed = sem("earlier_landed")
        cleared = [sem(f"cleared{a}") for a in range(TILES)]
        settled = [sem(f"settled{a}") for a in range(TILES)]
        more_loaded = [sem(f"more_loaded{k}") for k in range(TILES - FEW)]
        more_added = sem("more_added")
        parts_loaded = pair(lambda u: sem(f"parts_loaded{u}"))
        whole_done = sem("whole_done")
        side_done = sem("side_done")
        y_done = sem("y_done")
        normal_done = sem("normal_done")
        out_ready = sem("out_ready")
        out_stored = sem("out_stored")

        def node_rows(t):
            return t.rearrange("(p w) d -> p w d", p=P)

        cuts = [0, *range(BATCH - 2, W, BATCH), W]
        BATCHES = [slice(*ends) for ends in zip(cuts, cuts[1:])]
        QUARTERS = [slice(w0, min(w0 + 13, W)) for w0 in range(0, W, 13)]
        HALVES = [slice(0, 26), slice(26, W)]

        def size(part):
            return (part.stop - part.start) * D

        def flat(t):
            return t.rearrange("p w d -> p (w d)")

        def run_units(eng, step):
            for t in range(PEELED):
                step(t, 0)
            with eng.Fori(0, QUADS - 3) as r:
                for t in range(PEELED, PEELED + QUAD):
                    step(t, r)
            for t in range(UNITS - QUAD, UNITS):
                step(t, 0)

        def uses(t, r):
            return 2 * r + t // 2

        def later_quad(t, r):
            return t >= QUAD or not isinstance(r, int)

        def clear(eng, a, part=slice(0, W)):
            eng.dma_start(node_rows(sums_dram[a])[:, part], zeros[:].rearrange("p (w d) -> p w d", d=D)[:, part]
                          ).then_inc(cleared[a], 16)

        def choose(eng, edges):
            eng.wait_ge(way_ready, 1)
            indirect = eng.value_load(scattered[0:1, 0:1], min_val=0, max_val=1)
            with eng.If(indirect == 0):
                edges(True)
            with eng.Else():
                edges(False)

        block = ctx.enter_context(nc.Block())

        @block.sync
        def _(sp):
            for u in range(2):
                sp.dma_start(x[:, HALVES[u]], node_rows(x_in)[:, HALVES[u]]).then_inc(x_loaded[u], 16)
            sp.dma_start(ids[:], rows_in).then_inc(ids_loaded, 16)

            def load(t, r=0):
                u, g = t % 2, QUAD * r + t
                sp.dma_start(index[u][:], index_in[g]).then_inc(index_loaded[u], 16)
                sp.dma_start(attr[u][:], attr_in[g]).then_inc(attr_loaded[u], 16)

            def load_rows(t, r=0):
                u, g = t % 2, QUAD * r + t
                sp.dma_start(rows[u][:].rearrange("p j e -> p (j e)"),
                             rows_dram[bass.ds(g, 1)].to_broadcast([P, 2 * TILES * P])).then_inc(rows_loaded[u], 16)

            def buffers_free(t, r, windowed):
                u, n = t % 2, uses(t, r)
                if not windowed:
                    sp.wait_ge(gather_done[u], 16 * TILES * n)
                sp.wait_ge(src_ready[u], n)
                sp.wait_ge(match_built[u], n)
                sp.wait_ge(mlp1_done[u], n)
                sp.sem_inc(load_go, 1)

            def load_window(t, r=0):
                u, n = t % 2, uses(t, r)
                sp.wait_ge(index_loaded[u], 16 * (n + 1))
                sp.wait_ge(picked[u], n)
                sp.sem_inc(window_go, 1)
                first = sp.value_load(index[u][0:1, TILES:TILES + 1], min_val=0, max_val=NODES - 1)
                sp.dma_start(window[u][:], wxh_dram[bass.ds(first, P), :]).then_inc(window_loaded[u], 16)

            load(0)
            load(1)
            sp.wait_ge(zeros_ready, 1)
            clear(sp, 0)
            sp.wait_ge(ids16_ready, 2)
            sp.dma_start(rows_dram.rearrange("(b u) e -> b (u e)", u=2),
                         ids16[:].rearrange("b u j e -> b (u j e)")).then_inc(rows_stored, 16)
            clear(sp, 1)
            sp.wait_ge(rows_stored, 16)
            load_rows(0)
            load_rows(1)
            for n, part in enumerate(BATCHES):
                sp.wait_ge(wxh_ready, n + 1)
                sp.dma_start(node_rows(wxh_dram)[:, part], square[:, part]).then_inc(wxh_stored, 16)
            for part in QUARTERS[:2]:
                clear(sp, 2, part)
            sp.wait_ge(wxh_stored, 16 * len(BATCHES))

            def edges(windowed):
                if windowed:
                    load_window(0)
                    load_window(1)
                for part in QUARTERS[2:]:
                    clear(sp, 2, part)
                clear(sp, 3)

                def step(t, r):
                    buffers_free(t, r, windowed)
                    load(t, r)
                    load_rows(t, r)
                    if windowed:
                        load_window(t, r)

                pieces = [(a, part) for a in range(FEW, TILES) for part in QUARTERS]
                for t in range(2, PEELED):
                    step(t, 0)
                    for n in range(3 * (t - 2), min(3 * (t - 1), len(pieces))):
                        sp.wait_ge(scatter_go, 2 * n + 1)
                        clear(sp, *pieces[n])
                with sp.Fori(0, QUADS - 2) as r:
                    for t in range(PEELED, PEELED + QUAD):
                        step(t, r)

            choose(sp, edges)

            for a in range(FEW, TILES):
                sp.wait_ge(settled[a], landings(a, UNITS))
            piece = 0
            for k, a in enumerate(range(FEW, TILES)):
                for part in QUARTERS:
                    pace = 3 * piece // 2
                    sp.wait_ge(settled[pace % FEW], landings(pace % FEW, UNITS - QUAD) + 16 * (pace // FEW + 1))
                    sp.dma_start(more[k][:, part], node_rows(sums_dram[a])[:, part]).then_inc(more_loaded[k], 16)
                    piece += 1

            def load_parts(n, accumulators):
                part = BATCHES[n]
                for a in accumulators:
                    sp.dma_start(parts[n % 2][:, a, 0:part.stop - part.start], node_rows(sums_dram[a])[:, part]
                                 ).then_inc(parts_loaded[n % 2], 16)

            last = {a for _, a in scatters(UNITS - 1)}
            for ready in (set(range(FEW)) - last, last):
                for a in sorted(ready):
                    sp.wait_ge(settled[a], landings(a, UNITS))
                for n in range(2):
                    load_parts(n, sorted(ready))
            for n in range(2, len(BATCHES)):
                sp.wait_ge(whole_done, n - 1)
                sp.wait_ge(side_done, n - 1)
                load_parts(n, range(FEW))

        @block.gpsimd
        def _(pool):
            steps = [0]

            def then_next(ins):
                steps[0] += 1
                ins.then_inc(pool_step, 1)
                pool.wait_ge(pool_step, steps[0])

            nc.gpsimd.memset(eps[:], EPS).then_inc(eps_ready, 1)
            nc.gpsimd.memset(zeros[:], 0.0).then_inc(zeros_ready, 1)

            pool.wait_ge(ids_loaded, 16)
            nc.gpsimd.tensor_copy(ids16[:, 1], ids[:, 1]).then_inc(ids16_ready, 1)
            pool.wait_ge(centred, len(HALVES))
            pool.wait_ge(const_loaded, 32)
            nc.gpsimd.tensor_tensor(x[:], x[:], beta.rearrange("p (o d) -> p o d", o=1).to_broadcast([P, W, D]),
                                    ALU.add).then_inc(x_beta_done, 1)

            def gather(t, r):
                u, n = t % 2, uses(t, r)
                pool.wait_ge(index_loaded[u], 16 * (n + 1))
                pool.wait_ge(sum_done[u], n)
                pool.sem_inc(gather_go, 1)
                for j in range(TILES):
                    pool.indirect_dma_start(
                        gathered[u][:, j], None, wxh_dram,
                        bass.IndirectOffsetOnAxis(ap=index[u][:, TILES + j:TILES + j + 1].bitcast(U32), axis=0),
                    ).then_inc(gather_done[u], 16)

            def scatter(t, r):
                u, slot = t % 2, t % QUAD
                pool.wait_ge(target_ready[u], uses(t, r) + 1)
                pool.wait_ge(sum_copied, QUAD * r + t + 1)
                tiles = scatters(t)
                taken = [0] * TILES
                for k, (j, a) in enumerate(tiles):
                    if t < PEELED:
                        pool.wait_ge(cleared[a], 16 * (len(QUARTERS) if a in (2, *range(FEW, TILES)) else 1))
                    pool.wait_ge(settled[a], 16 * QUAD * r + landings(a, t) + 16 * taken[a])
                    taken[a] += 1
                    pool.sem_inc(scatter_go if k < len(tiles) - 1 else earlier_landed, 1)
                    pool.indirect_dma_start(
                        sums_dram[a], bass.IndirectOffsetOnAxis(ap=target[slot][:, j:j + 1], axis=0),
                        summed[slot][:, j], None, compute_op=ALU.add).then_inc(settled[a], 16)

            pool.wait_ge(wxh_stored, 16 * len(BATCHES))

            def edges(windowed):
                def step(t, r):
                    if not windowed:
                        if t == 0:
                            gather(0, 0)
                        if t + 1 < UNITS:
                            gather(t + 1, r)
                    scatter(t, r)

                run_units(pool, step)

            choose(pool, edges)

            def finish(n):
                part = BATCHES[n]
                cols = part.stop - part.start
                pool.wait_ge(normal_done, n + 1)
                then_next(nc.gpsimd.tensor_tensor(work[:, part], work[:, part],
                                                  gamma.rearrange("p (o d) -> p o d", o=1)
                                                  .to_broadcast([P, cols, D]), ALU.mult))
                nc.gpsimd.tensor_tensor(work[:, part], work[:, part], x[:, part], ALU.add).then_inc(out_ready, 1)

            pool.wait_ge(x_beta_done, 1)
            for n, part in enumerate(BATCHES):
                cols = part.stop - part.start
                pool.wait_ge(parts_loaded[n % 2], 16 * FEW * (n // 2 + 1))
                if n >= 2:
                    pool.wait_ge(y_done, n - 1)
                nc.gpsimd.tensor_tensor(side[n % 2][:, 0:cols], parts[n % 2][:, 2, 0:cols],
                                        parts[n % 2][:, 3, 0:cols], ALU.add).then_inc(side_done, 1)
                if n >= 2:
                    finish(n - 2)
            finish(len(BATCHES) - 2)
            finish(len(BATCHES) - 1)

        def project(pe, n):
            cols = size(BATCHES[n])
            pe.wait_ge(hT_ready, n + 1)
            if n >= 2:
                pe.wait_ge(wxh_ready, n - 1)
            for k in range(cols // P):
                last = nc.tensor.matmul([ps_hidden, ps_filter][n % 2][:, k * P:(k + 1) * P],
                                        hT[n % 2][:, k * P:(k + 1) * P], wl, start=True, stop=True)
            last.then_inc(wxh_done, 1)

        def enter_unit(pe, t, r=0):
            u, b = t % 2, uses(t, r)
            pe.wait_ge(attr_loaded[u], 16 * (b + 1))
            pe.wait_ge(silu_done[1 - u], b + u)
            nc.tensor.matmul(ps_hidden[:], w1, attr[u][:], start=True, stop=True).then_inc(mlp1_done[u], 1)

        def pick(pe, t, r):
            u, b = t % 2, uses(t, r)
            pe.wait_ge(picked_copied[1 - u], b + u)
            pe.wait_ge(window_loaded[u], 16 * (b + 1))
            pe.wait_ge(onehot_built[u], b + 1)
            for j in range(TILES):
                last = nc.tensor.matmul(ps_gather[:, j * D:(j + 1) * D], onehot[u][:, j], window[u][:],
                                        start=True, stop=True)
            last.then_inc(picked[u], 1)

        def filter_edges(pe, t, r):
            u, b, g = t % 2, uses(t, r), QUAD * r + t
            pe.wait_ge(filter_read, g)
            pe.wait_ge(silu_done[u], b + 1)
            for k in range(CHUNKS):
                last = nc.tensor.matmul(ps_filter[:, k * P:(k + 1) * P], hidden[u][:, k * P:(k + 1) * P], w2,
                                        start=True, stop=True)
            last.then_inc(filter_done[u], 1)

        def leave_unit(pe, t, r=0):
            u, b, g = t % 2, uses(t, r), QUAD * r + t
            pe.wait_ge(sum_copied, g)
            pe.wait_ge(msg_done, g + 1)
            pe.wait_ge(match_built[u], b + 1)
            for j in range(TILES):
                last = nc.tensor.matmul(ps_sum[:, j * D:(j + 1) * D], last_match[u][:, j], msg[u][:, j],
                                        start=True, stop=True)
            last.then_inc(sum_done[u], 1)

        @block.tensor
        def _(pe):
            pe.wait_ge(const_loaded, 32)
            pe.wait_ge(first_ready, 1)
            for u in range(2):
                last = nc.tensor.transpose(ps_first[:, u * BLOCKS:(u + 1) * BLOCKS],
                                           dst_first[:, u:u + 1].to_broadcast([BLOCKS, P]),
                                           ident[0:BLOCKS, 0:BLOCKS])
            last.then_inc(first_spread, 1)
            for n, part in enumerate(BATCHES):
                pe.wait_ge(h_ready, n + 1)
                if n >= 2:
                    pe.wait_ge(hT_ready, n - 1)
                for k in range(size(part) // P):
                    last = nc.tensor.transpose(ps_turn[n % 2][:, k * P:(k + 1) * P],
                                               flat(h[:, part.start + 2 * k:part.start + 2 * k + 2, :]), ident)
                last.then_inc(h_turned, 1)
                if n >= 1:
                    project(pe, n - 1)
            project(pe, len(BATCHES) - 1)
            pe.wait_ge(wxh_ready, len(BATCHES))

            enter_unit(pe, 0)
            pe.wait_ge(far_ready, 1)
            nc.tensor.transpose(ps_far[0:1, 0:BLOCKS], dst_far[:], ident[0:BLOCKS, 0:BLOCKS]).then_inc(far_turned, 1)
            filter_edges(pe, 0, 0)
            enter_unit(pe, 1)

            def edges(windowed):
                def step(t, r):
                    if t == 0:
                        if windowed:
                            pick(pe, 0, 0)
                        leave_unit(pe, 0)
                        return
                    if windowed:
                        pick(pe, t, r)
                    filter_edges(pe, t, r)
                    if t >= 2:
                        leave_unit(pe, t - 1, r)
                    if t + 1 < UNITS:
                        enter_unit(pe, t + 1, r)

                run_units(pe, step)
                leave_unit(pe, UNITS - 1)

            choose(pe, edges)

            for n, part in enumerate(BATCHES):
                cols = size(part)
                if n >= 2:
                    pe.wait_ge(y_done, n - 1)
                pe.wait_ge(more_added, n + 1)
                total = [ps_hidden, ps_filter][n % 2][:, 0:cols]
                nc.tensor.matmul(total, ident, flat(h[:, part]), start=True, stop=False)
                pe.wait_ge(parts_loaded[n % 2], 16 * FEW * (n // 2 + 1))
                for a in range(2):
                    last = nc.tensor.matmul(total, ident, flat(parts[n % 2][:, a, 0:cols // D]),
                                            start=False, stop=(a == 1))
                last.then_inc(whole_done, 1)

        @block.scalar
        def _(act):
            act.dma_start(const[:], const_in).then_inc(const_loaded, 16)
            act.dma_start(value[:], value_in).then_inc(const_loaded, 16)
            for n, half in enumerate(HALVES):
                act.wait_ge(centred, n + 1)
                nc.scalar.activation(square[:, half], work[:, half], ACT.Square).then_inc(squared, 1)
            act.wait_ge(variance, 1)
            act.wait_ge(eps_ready, 1)
            nc.scalar.activation(stat[:, 3], stat[:, 2], ACT.Sqrt, bias=eps[:], scale=1.0 / D).then_inc(deviation, 1)
            act.wait_ge(ids_loaded, 16)
            nc.scalar.copy(ids16[:, 0], ids[:, 0]).then_inc(ids16_ready, 1)
            for n, part in enumerate(BATCHES):
                cols = size(part)
                act.wait_ge(h_turned, n + 1)
                if n >= 2:
                    act.wait_ge(wxh_done, n - 1)
                nc.scalar.copy(hT[n % 2][:, :cols], ps_turn[n % 2][:, :cols]).then_inc(hT_ready, 1)
            nc.scalar.activation(silu_first[:], eps[:], ACT.Silu)

            def silu(t, r=0):
                u, b = t % 2, uses(t, r)
                act.wait_ge(mlp1_done[u], b + 1)
                act.wait_ge(filter_done[u], b)
                nc.scalar.activation(hidden[u][:], ps_hidden[:], ACT.Silu, bias=b1).then_inc(silu_done[u], 1)

            def copy_picked(t, r):
                u, b = t % 2, uses(t, r)
                act.wait_ge(picked[u], b + 1)
                act.wait_ge(sum_done[u], b)
                nc.scalar.copy(gathered[u][:].rearrange("p j d -> p (j d)"), ps_gather[:]
                               ).then_inc(picked_copied[u], 1)

            def copy_sum(t, r=0):
                u, b, g = t % 2, uses(t, r), QUAD * r + t
                act.wait_ge(sum_done[u], b + 1)
                if later_quad(t, r):
                    act.wait_ge(earlier_landed, g - QUAD + 2)
                nc.scalar.copy(summed[t % QUAD][:].rearrange("p j d -> p (j d)"), ps_sum[:]).then_inc(sum_copied, 1)

            silu(0)
            silu(1)

            def edges(windowed):
                def step(t, r):
                    if windowed:
                        copy_picked(t, r)
                    if t == 0:
                        copy_sum(0)
                        return
                    if t >= 2:
                        copy_sum(t - 1, r)
                    if t + 1 < UNITS:
                        silu(t + 1, r)

                run_units(act, step)
                copy_sum(UNITS - 1)

            choose(act, edges)

            def store(n):
                act.wait_ge(out_ready, n + 1)
                act.dma_start(node_rows(out)[:, BATCHES[n]], work[:, BATCHES[n]]).then_inc(out_stored, 16)

            for n, part in enumerate(BATCHES):
                act.wait_ge(centred, len(HALVES) + n + 1)
                nc.scalar.activation(square[:, part], work[:, part], ACT.Square).then_inc(squared, 1)
                act.wait_ge(variance, n + 2)
                nc.scalar.activation(stat[:, 3, part], stat[:, 2, part], ACT.Sqrt, bias=eps[:],
                                     scale=1.0 / D).then_inc(deviation, 1)
                if n >= 2:
                    store(n - 2)
            store(len(BATCHES) - 2)
            store(len(BATCHES) - 1)
            act.wait_ge(out_stored, 16 * len(BATCHES))

        @block.vector
        def _(dve):
            steps = [0]

            def then_next(ins):
                steps[0] += 1
                ins.then_inc(ln_step, 1)
                dve.wait_ge(ln_step, steps[0])

            def wide(column, n):
                return column.rearrange("p (w o) -> p w o", o=1).to_broadcast([P, n, D])

            def centre(part, y):
                then_next(nc.vector.tensor_reduce(stat[:, 0, part], y, AX_X, ALU.add))
                then_next(nc.vector.tensor_scalar(stat[:, 1, part], stat[:, 0, part], -1.0 / D, None, ALU.mult))
                return nc.vector.tensor_tensor(work[:, part], y, wide(stat[:, 1, part], part.stop - part.start),
                                               ALU.add)

            for n, half in enumerate(HALVES):
                dve.wait_ge(x_loaded[n], 16)
                centre(half, x[:, half]).then_inc(centred, 1)
            first, low, high, most = dst_first[:], dst_span[:, 0, :], dst_span[:, 1, :], dst_span[:, 2, :]
            dst = ids[:, :, TILES:2 * TILES, :].rearrange("b u j e -> b u (j e)")
            dve.wait_ge(ids_loaded, 16)
            nc.vector.tensor_copy(first, dst[:, :, 0]).then_inc(first_ready, 1)
            for n, half in enumerate(HALVES):
                dve.wait_ge(squared, n + 1)
                last = nc.vector.tensor_reduce(stat[:, 2, half], square[:, half], AX_X, ALU.add)
            last.then_inc(variance, 1)
            dve.wait_ge(deviation, 1)
            then_next(nc.vector.reciprocal(stat[:, 0], stat[:, 3]))
            for part in BATCHES:
                nc.vector.scalar_tensor_tensor(out=h[:, part], in0=work[:, part], scalar=0.0,
                                               in1=wide(stat[:, 0, part], part.stop - part.start),
                                               op0=ALU.max, op1=ALU.mult).then_inc(h_ready, 1)
            for n, part in enumerate(BATCHES):
                dve.wait_ge(wxh_done, n + 1)
                nc.vector.tensor_tensor(square[:, part], [ps_hidden, ps_filter][n % 2][:, 0:size(part)]
                                        .rearrange("p (w d) -> p w d", d=D),
                                        bl.rearrange("p (o d) -> p o d", o=1)
                                        .to_broadcast([P, part.stop - part.start, D]), ALU.add
                                        ).then_inc(wxh_ready, 1)
                if n == len(BATCHES) // 2:
                    nc.vector.tensor_reduce(low, dst, AX_X, ALU.min)
            then_next(nc.vector.tensor_reduce(high, dst, AX_X, ALU.max))
            dve.wait_ge(first_ready, 1)
            then_next(nc.vector.tensor_tensor(low, first, low, ALU.subtract))
            then_next(nc.vector.scalar_tensor_tensor(out=high, in0=high, scalar=1.0 - P, in1=first,
                                                     op0=ALU.add, op1=ALU.subtract))
            then_next(nc.vector.tensor_tensor(most, low, high, ALU.max))
            nc.vector.tensor_reduce(dst_far[:], most, AX_X, ALU.max).then_inc(far_ready, 1)
            dve.wait_ge(const_loaded, 32)
            dve.wait_ge(first_spread, 1)
            nc.vector.tensor_scalar(window_rows[:].rearrange("p u b -> p (u b)"), ps_first[:, 0:2 * BLOCKS],
                                    place, None, ALU.add).then_inc(window_rows_ready, 1)
            dve.wait_ge(far_turned, 1)
            then_next(nc.vector.tensor_reduce(dst_first[0:1, 0:1], ps_far[0:1, 0:BLOCKS], AX_X, ALU.max))
            nc.vector.tensor_scalar(scattered[:], dst_first[0:1, 0:1], 0.0, None, ALU.is_gt
                                    ).then_inc(way_ready, 1)

            def src_columns(t, r):
                u, b = t % 2, uses(t, r)
                dve.wait_ge(index_loaded[u], 16 * (b + 1))
                dve.wait_ge(target_ready[u], b)
                nc.vector.tensor_copy(src[u][:], index[u][:, 0:TILES]).then_inc(src_ready[u], 1)

            def onehots(t, r):
                u, b = t % 2, uses(t, r)
                dve.wait_ge(picked[u], b)
                dve.wait_ge(rows_loaded[u], 16 * (b + 1))
                nc.vector.tensor_scalar(onehot[u][:].rearrange("p j e -> p (j e)"),
                                        rows[u][:, TILES:2 * TILES, :].rearrange("p j e -> p (j e)"),
                                        window_rows[:, u, bass.ds(b, 1)], None, ALU.is_equal
                                        ).then_inc(onehot_built[u], 1)

            def last_matches(t, r):
                u, b = t % 2, uses(t, r)
                dve.wait_ge(rows_loaded[u], 16 * (b + 1))
                dve.wait_ge(src_ready[u], b + 1)
                dve.wait_ge(sum_done[u], b)
                for j in range(TILES):
                    last = nc.vector.scalar_tensor_tensor(
                        out=last_match[u][:, j], in0=rows[u][:, j, :],
                        scalar=src[u][:, j:j + 1], in1=mask, op0=ALU.is_equal, op1=ALU.mult,
                        accum_out=matches[u][:, j:j + 1])
                last.then_inc(match_built[u], 1)

            def prepare(t, r, windowed):
                src_columns(t, r)
                if windowed:
                    onehots(t, r)
                last_matches(t, r)

            def messages(t, r, windowed):
                u, b = t % 2, uses(t, r)
                dve.wait_ge(filter_done[u], b + 1)
                dve.wait_ge(sum_done[u], b)
                nc.vector.tensor_tensor(msg[u][:], ps_filter[:].rearrange("p (j d) -> p j d", d=D),
                                        b2.rearrange("p (o d) -> p o d", o=1).to_broadcast([P, TILES, D]), ALU.add
                                        ).then_inc(filter_read, 1)
                dve.wait_ge(filter_read, QUAD * r + t + 1)
                if windowed:
                    dve.wait_ge(picked_copied[u], b + 1)
                else:
                    dve.wait_ge(gather_done[u], 16 * TILES * (b + 1))
                nc.vector.tensor_tensor(msg[u][:], msg[u][:], gathered[u][:], ALU.mult).then_inc(msg_done, 1)

            def targets(t, r=0):
                u, b, g = t % 2, uses(t, r), QUAD * r + t
                dve.wait_ge(match_built[u], b + 1)
                nc.vector.tensor_scalar(spare[u][:], matches[u][:], 1.0, spare_row, ALU.is_gt,
                                        ALU.mult).then_inc(spare_done, 1)
                dve.wait_ge(spare_done, g + 1)
                if later_quad(t, r):
                    dve.wait_ge(earlier_landed, g - QUAD + 2)
                nc.vector.tensor_tensor(target[t % QUAD][:], spare[u][:], src[u][:], ALU.max
                                        ).then_inc(target_ready[u], 1)

            src_columns(0, 0)
            src_columns(1, 0)

            def edges(windowed):
                def step(t, r):
                    if t == 0:
                        if windowed:
                            dve.wait_ge(window_rows_ready, 1)
                            onehots(0, 0)
                            onehots(1, 0)
                        last_matches(0, 0)
                        last_matches(1, 0)
                    messages(t, r, windowed)
                    if t == 0:
                        targets(0)
                        return
                    if t >= 2:
                        targets(t - 1, r)
                    if t + 1 < UNITS:
                        prepare(t + 1, r, windowed)

                run_units(dve, step)
                targets(UNITS - 1)

            choose(dve, edges)

            for k in range(TILES - FEW):
                dve.wait_ge(more_loaded[k], 16 * len(QUARTERS))
                if k < TILES - FEW - 1:
                    then_next(nc.vector.tensor_tensor(h[:], h[:], more[k], ALU.add))
                else:
                    for part in BATCHES:
                        nc.vector.tensor_tensor(h[:, part], h[:, part], more[k][:, part], ALU.add
                                                ).then_inc(more_added, 1)

            def add_up(n):
                part = BATCHES[n]
                dve.wait_ge(whole_done, n + 1)
                dve.wait_ge(side_done, n + 1)
                nc.vector.tensor_tensor(flat(h[:, part]), [ps_hidden, ps_filter][n % 2][:, 0:size(part)],
                                        flat(side[n % 2][:, 0:part.stop - part.start]), ALU.add
                                        ).then_inc(y_done, 1)
                dve.wait_ge(y_done, n + 1)
                centre(part, h[:, part]).then_inc(centred, 1)

            def spread(n):
                part = BATCHES[n]
                dve.wait_ge(squared, len(HALVES) + n + 1)
                nc.vector.tensor_reduce(stat[:, 2, part], square[:, part], AX_X, ALU.add).then_inc(variance, 1)

            def normalise(n):
                part = BATCHES[n]
                dve.wait_ge(deviation, n + 2)
                then_next(nc.vector.reciprocal(stat[:, 0, part], stat[:, 3, part]))
                nc.vector.tensor_tensor(work[:, part], work[:, part], wide(stat[:, 0, part], part.stop - part.start),
                                        ALU.mult).then_inc(normal_done, 1)

            add_up(0)
            for n in range(1, len(BATCHES)):
                spread(n - 1)
                add_up(n)
                normalise(n - 1)
            spread(len(BATCHES) - 1)
            normalise(len(BATCHES) - 1)


def kernel(**inputs):
    import numpy as np
    import concourse.bacc as bacc
    from concourse.bass_utils import run_bass_kernel_spmd

    def get(name):
        return np.asarray(inputs[name])

    f32 = np.float32
    x = np.zeros((ROWS, D), f32)
    x[:NODES] = get("x")
    attr = np.zeros((UNITS * UNIT, D), f32)
    attr[:EDGES] = get("edge_attr_64")
    attr = np.ascontiguousarray(attr.reshape(UNITS, 2, HALF, D).transpose(0, 1, 3, 2)).reshape(UNITS, P, HALF)

    def by_tile(ids, fill):
        padded = fill.astype(np.int32)
        padded[:EDGES] = ids
        return padded.reshape(UNITS, 2, CHUNKS, P).transpose(0, 3, 2, 1).reshape(UNITS, P, TILES)

    places = np.arange(UNITS * UNIT)
    index = np.ascontiguousarray(np.concatenate(
        [by_tile(get("src"), NODES + places % P), by_tile(get("dst"), np.full_like(places, NODES - 1))], axis=2))

    rows = np.ascontiguousarray(index.transpose(0, 2, 1)).reshape(BLOCKS, 2, 2 * TILES, P)

    const = np.zeros((P, CONST_COLS), f32)
    const[:, C_PLACE] = np.arange(P)
    const[:, C_IDENT:C_IDENT + P] = np.eye(P)
    const[:, C_MASK:C_MASK + P] = np.triu(np.ones((P, P)))
    const[:, C_SPARE] = NODES + np.arange(P)

    value = np.zeros((P, VALUE_COLS), f32)
    for at, name in ((V_W1, "L0_gnn_Wf1"), (V_W2, "L0_gnn_Wf2"), (V_WL, "L0_gnn_Wl")):
        value[:D, at:at + D] = get(name).T
        value[D:, at + D:at + P] = get(name).T
    value[:, V_GAMMA:V_GAMMA + D] = get("L0_gnn_gamma")
    value[:, V_BETA:V_BETA + D] = get("L0_gnn_beta")
    value[:D, V_B1] = get("L0_gnn_bf1")
    value[D:, V_B1] = get("L0_gnn_bf1")

    value[:, V_BL:V_BL + D] = get("L0_gnn_bl")
    value[:, V_B2:V_B2 + D] = get("L0_gnn_bf2")

    nc = bacc.Bacc("TRN2", target_bir_lowering=False, num_devices=1)
    arrays = {"x_in": x, "attr_in": attr, "index_in": index, "rows_in": rows,
              "const_in": const, "value_in": value}
    args = [nc.dram_tensor(name, a.shape, mybir.dt.from_np(a.dtype), kind="ExternalInput").ap()
            for name, a in arrays.items()]
    out = nc.dram_tensor("out_rows", (ROWS, D), F32, kind="ExternalOutput").ap()
    build(nc, *args, out)
    result = run_bass_kernel_spmd(nc, [arrays], core_ids=[0])
    return result.results[0]["out_rows"][:NODES]
```
